# Optimizing a Trainium2 kernel written in Bass

```python
import numpy as np
import jax
import jax.numpy as jnp

def _softmax(x, axis=-1):
    return jax.nn.softmax(x, axis=axis)

def _gelu(x):
    return jax.nn.gelu(x, approximate=True)

def _silu(x):
    return jax.nn.silu(x)

def _sigmoid(x):
    return jax.nn.sigmoid(x)

def _layernorm(x, axis=-1, eps=1e-05):
    m = jnp.mean(x, axis=axis, keepdims=True)
    v = jnp.var(x, axis=axis, keepdims=True)
    return (x - m) / jnp.sqrt(v + eps)

def _scatter_add(tgt, idx, src, axis=0):
    return tgt.at[idx].add(src)

def _segment_sum(src, seg, n):
    return jax.ops.segment_sum(src, seg, n)
kernel_name = 'mk_gnn_preln_d4_gnn_r32_c1ab6c'

def setup_inputs(seed: int=0):
    np.random.seed(seed)
    _w = jnp.asarray

    def _rec_inputs():
        import jax
        import jax.numpy as jnp
        _gk = jax.random.key(seed)
        x = -0.0003713 + 1 * jax.random.normal(jax.random.fold_in(_gk, 1), (3125, 128), jnp.float32)
        _s = jax.random.randint(jax.random.fold_in(_gk, 2), (50000,), 0, 3125, jnp.int32)
        _d = jax.random.randint(jax.random.fold_in(_gk, 3), (50000,), 0, 3125, jnp.int32)
        _loop = jnp.arange(3125, dtype=jnp.int32)
        src = jnp.concatenate([_s, _d, _loop])
        dst = jnp.concatenate([_d, _s, _loop])
        _o = jnp.argsort(dst, stable=True)
        src = src[_o]
        dst = dst[_o]
        edge_type_8 = jax.random.randint(jax.random.fold_in(_gk, 13), (103125,), 0, 8, jnp.int32)
        return (x, src, dst, edge_type_8)
    x, src, dst, edge_type_8 = _rec_inputs()

    def _L0_gnn_setup():
        import jax, jax.numpy as jnp
        import numpy as np
        N_NODES = 3125
        N_EDGES = 50000
        D_IN = 128
        D_OUT = 128
        EPS = 1e-05
        key = jax.random.key(seed)
        ks = jax.random.split(key, 5)
        x = jax.random.normal(ks[0], (N_NODES, D_IN), dtype=jnp.float32)
        edge_index = jax.random.randint(ks[1], (2, N_EDGES), 0, N_NODES, dtype=jnp.int64)
        scale = 1.0 / np.sqrt(D_IN)
        W_root = jax.random.normal(ks[2], (D_IN, D_OUT), dtype=jnp.float32) * scale
        W_rel = jax.random.normal(ks[3], (D_IN, D_OUT), dtype=jnp.float32) * scale
        b_rel = jax.random.normal(ks[4], (D_OUT,), dtype=jnp.float32) * 0.01
        gamma = jnp.ones((D_OUT,), dtype=jnp.float32)
        beta = jnp.zeros((D_OUT,), dtype=jnp.float32)
        return {'x': x, 'edge_index': edge_index, 'W_root': W_root, 'W_rel': W_rel, 'b_rel': b_rel, 'gamma': gamma, 'beta': beta}
    _L0_gnn_all = _L0_gnn_setup()
    _L0_gnn_in = {k: v for k, v in _L0_gnn_all.items() if k in ('W_root', 'W_rel', 'b_rel', 'gamma', 'beta')}
    del _L0_gnn_all

    def _L1_gnn_setup():
        import jax, jax.numpy as jnp
        import numpy as np
        N_NODES = 50000
        N_EDGES = 25000
        D_IN = 128
        D_HID = 128
        key = jax.random.key(seed)
        ks = jax.random.split(key, 9)
        s_in = 1.0 / np.sqrt(D_IN)
        s_hid = 1.0 / np.sqrt(D_HID)
        return {'x': jax.random.normal(ks[0], (N_NODES, D_IN), dtype=jnp.float32), 'W_self0': jax.random.normal(ks[1], (D_HID, D_IN), dtype=jnp.float32) * s_in, 'W_neigh0': jax.random.normal(ks[2], (D_HID, D_IN), dtype=jnp.float32) * s_in, 'b0': jnp.zeros((D_HID,), dtype=jnp.float32), 'W_self1': jax.random.normal(ks[3], (D_HID, D_HID), dtype=jnp.float32) * s_hid, 'W_neigh1': jax.random.normal(ks[4], (D_HID, D_HID), dtype=jnp.float32) * s_hid, 'b1': jnp.zeros((D_HID,), dtype=jnp.float32), 'edge_src': jax.random.randint(ks[5], (N_EDGES,), 0, N_NODES, dtype=jnp.int32), 'edge_dst': jax.random.randint(ks[6], (N_EDGES,), 0, N_NODES, dtype=jnp.int32)}
    _L1_gnn_all = _L1_gnn_setup()
    _L1_gnn_in = {k: v for k, v in _L1_gnn_all.items() if k in ('W_self0', 'W_neigh0', 'b0', 'W_self1', 'W_neigh1', 'b1')}
    del _L1_gnn_all

    def _L2_gnn_setup():
        import jax, jax.numpy as jnp
        import numpy as np
        N, E, DIM, HEADS = (1250, 20000, 128, 8)
        HD = DIM // HEADS
        NEG_SLOPE = 0.2
        key = jax.random.key(seed)
        ks = jax.random.split(key, 10)
        s = 1.0 / np.sqrt(DIM)
        return {'x': jax.random.normal(ks[0], (N, DIM), dtype=jnp.float32), 'edge_index': jax.random.randint(ks[1], (2, E), 0, N, dtype=jnp.int64), 'W_src': jax.random.normal(ks[2], (DIM, DIM), dtype=jnp.float32) * s, 'b_src': jnp.zeros((DIM,), dtype=jnp.float32), 'W_dst': jax.random.normal(ks[3], (DIM, DIM), dtype=jnp.float32) * s, 'b_dst': jnp.zeros((DIM,), dtype=jnp.float32), 'att': jax.random.normal(ks[4], (HEADS, HD), dtype=jnp.float32) * (1.0 / np.sqrt(HD)), 'bias_out': jnp.zeros((DIM,), dtype=jnp.float32), 'ln_gamma': jnp.ones((DIM,), dtype=jnp.float32), 'ln_beta': jnp.zeros((DIM,), dtype=jnp.float32)}
    _L2_gnn_all = _L2_gnn_setup()
    _L2_gnn_in = {k: v for k, v in _L2_gnn_all.items() if k in ('W_src', 'b_src', 'W_dst', 'b_dst', 'att', 'bias_out', 'ln_gamma', 'ln_beta')}
    del _L2_gnn_all

    def _L3_gnn_setup():
        import jax, jax.numpy as jnp
        import numpy as np
        N_ENT = 3125

        def _rgcn_layer(x, W, SW, b, src, dst, rel):
            xt = jnp.einsum('nd,rde->rne', x, W)
            msg = xt[rel, src]
            agg = jax.ops.segment_sum(msg, dst, num_segments=x.shape[0])
            return jax.nn.relu(agg + x @ SW + b)
        key = jax.random.key(seed)
        ks = jax.random.split(key, 8)
        d, R, E = (128, 8, 18750)
        scale = 1.0 / np.sqrt(d)
        return {'entity_emb': jax.random.normal(ks[0], (N_ENT, d), dtype=jnp.float32), 'w1': jax.random.normal(ks[1], (R, d, d), dtype=jnp.float32) * scale, 'sl1': jax.random.normal(ks[2], (d, d), dtype=jnp.float32) * scale, 'b1': jnp.zeros((d,), dtype=jnp.float32), 'w2': jax.random.normal(ks[3], (R, d, d), dtype=jnp.float32) * scale, 'sl2': jax.random.normal(ks[4], (d, d), dtype=jnp.float32) * scale, 'b2': jnp.zeros((d,), dtype=jnp.float32), 'edge_index': jax.random.randint(ks[5], (2, E), 0, N_ENT, dtype=jnp.int64), 'edge_type': jax.random.randint(ks[6], (E,), 0, R, dtype=jnp.int64)}
    _L3_gnn_all = _L3_gnn_setup()
    _L3_gnn_in = {k: v for k, v in _L3_gnn_all.items() if k in ('w1', 'sl1', 'b1', 'w2', 'sl2', 'b2')}
    del _L3_gnn_all
    return {'x': x, 'src': src, 'dst': dst, 'edge_type_8': edge_type_8, 'L0_gnn_W_root': _L0_gnn_in['W_root'], 'L0_gnn_W_rel': _L0_gnn_in['W_rel'], 'L0_gnn_b_rel': _L0_gnn_in['b_rel'], 'L0_gnn_gamma': _L0_gnn_in['gamma'], 'L0_gnn_beta': _L0_gnn_in['beta'], 'L1_gnn_W_self0': _L1_gnn_in['W_self0'], 'L1_gnn_W_neigh0': _L1_gnn_in['W_neigh0'], 'L1_gnn_b0': _L1_gnn_in['b0'], 'L1_gnn_W_self1': _L1_gnn_in['W_self1'], 'L1_gnn_W_neigh1': _L1_gnn_in['W_neigh1'], 'L1_gnn_b1': _L1_gnn_in['b1'], 'L2_gnn_W_src': _L2_gnn_in['W_src'], 'L2_gnn_b_src': _L2_gnn_in['b_src'], 'L2_gnn_W_dst': _L2_gnn_in['W_dst'], 'L2_gnn_b_dst': _L2_gnn_in['b_dst'], 'L2_gnn_att': _L2_gnn_in['att'], 'L2_gnn_bias_out': _L2_gnn_in['bias_out'], 'L2_gnn_ln_gamma': _L2_gnn_in['ln_gamma'], 'L2_gnn_ln_beta': _L2_gnn_in['ln_beta'], 'L3_gnn_w1': _L3_gnn_in['w1'], 'L3_gnn_sl1': _L3_gnn_in['sl1'], 'L3_gnn_b1': _L3_gnn_in['b1'], 'L3_gnn_w2': _L3_gnn_in['w2'], 'L3_gnn_sl2': _L3_gnn_in['sl2'], 'L3_gnn_b2': _L3_gnn_in['b2']}

def reference(x, src, dst, edge_type_8, L0_gnn_W_root, L0_gnn_W_rel, L0_gnn_b_rel, L0_gnn_gamma, L0_gnn_beta, L1_gnn_W_self0, L1_gnn_W_neigh0, L1_gnn_b0, L1_gnn_W_self1, L1_gnn_W_neigh1, L1_gnn_b1, L2_gnn_W_src, L2_gnn_b_src, L2_gnn_W_dst, L2_gnn_b_dst, L2_gnn_att, L2_gnn_bias_out, L2_gnn_ln_gamma, L2_gnn_ln_beta, L3_gnn_w1, L3_gnn_sl1, L3_gnn_b1, L3_gnn_w2, L3_gnn_sl2, L3_gnn_b2):
    import jax
    import jax.numpy as jnp

    def _L0_gnn_ref(x, edge_index, W_root, W_rel, b_rel, gamma, beta):
        import jax, jax.numpy as jnp
        import numpy as np
        N_NODES = 3125
        N_EDGES = 50000
        D_IN = 128
        D_OUT = 128
        EPS = 1e-05
        src = edge_index[0]
        dst = edge_index[1]
        aggr = jax.ops.segment_sum(x[src], dst, num_segments=x.shape[0])
        h = aggr @ W_rel + b_rel + x @ W_root
        mean = jnp.mean(h, axis=0)
        var = jnp.mean(jnp.square(h - mean), axis=0)
        h_norm = (h - mean) * jax.lax.rsqrt(var + EPS) * gamma + beta
        return jax.nn.relu(h_norm)

    def _L1_gnn_ref(x, W_self0, W_neigh0, b0, W_self1, W_neigh1, b1, edge_src, edge_dst):
        import jax, jax.numpy as jnp
        import numpy as np
        N_NODES = 50000
        N_EDGES = 25000
        D_IN = 128
        D_HID = 128
        N = x.shape[0]
        deg = jax.ops.segment_sum(jnp.ones(edge_dst.shape, dtype=x.dtype), edge_dst, num_segments=N)
        inv_deg = (1.0 / jnp.maximum(deg, 1.0))[:, None]

        def sage_conv(h, W_self, W_neigh, b):
            agg = jax.ops.segment_sum(h[edge_src], edge_dst, num_segments=N) * inv_deg
            return h @ W_self.T + agg @ W_neigh.T + b
        h = jax.nn.relu(sage_conv(x, W_self0, W_neigh0, b0))
        h = sage_conv(h, W_self1, W_neigh1, b1)
        return h

    def _L2_gnn_ref(x, edge_index, W_src, b_src, W_dst, b_dst, att, bias_out, ln_gamma, ln_beta):
        import jax, jax.numpy as jnp
        import numpy as np
        N, E, DIM, HEADS = (1250, 20000, 128, 8)
        HD = DIM // HEADS
        NEG_SLOPE = 0.2
        n = x.shape[0]
        loops = jnp.arange(n, dtype=edge_index.dtype)
        src = jnp.concatenate([edge_index[0], loops])
        dst = jnp.concatenate([edge_index[1], loops])
        xs = (x @ W_src + b_src).reshape(n, HEADS, HD)
        xd = (x @ W_dst + b_dst).reshape(n, HEADS, HD)
        e = xs[src] + xd[dst]
        e = jnp.where(e >= 0, e, NEG_SLOPE * e)
        logits = jnp.einsum('ehc,hc->eh', e, att)
        m = jax.ops.segment_max(logits, dst, num_segments=n)
        ex = jnp.exp(logits - m[dst])
        denom = jax.ops.segment_sum(ex, dst, num_segments=n)
        alpha = ex / denom[dst]
        msg = xs[src] * alpha[:, :, None]
        out = jax.ops.segment_sum(msg, dst, num_segments=n)
        out = out.reshape(n, DIM) + bias_out
        h = out + x
        mu = jnp.mean(h, axis=-1, keepdims=True)
        var = jnp.var(h, axis=-1, keepdims=True)
        h = (h - mu) / jnp.sqrt(var + 1e-05) * ln_gamma + ln_beta
        return jax.nn.gelu(h, approximate=False)

    def _L3_gnn_ref(entity_emb, w1, sl1, b1, w2, sl2, b2, edge_index, edge_type):
        import jax, jax.numpy as jnp
        import numpy as np
        N_ENT = 3125

        def _rgcn_layer(x, W, SW, b, src, dst, rel):
            xt = jnp.einsum('nd,rde->rne', x, W)
            msg = xt[rel, src]
            agg = jax.ops.segment_sum(msg, dst, num_segments=x.shape[0])
            return jax.nn.relu(agg + x @ SW + b)
        src, dst = (edge_index[0], edge_index[1])
        x = _rgcn_layer(entity_emb, w1, sl1, b1, src, dst, edge_type)
        x = _rgcn_layer(x, w2, sl2, b2, src, dst, edge_type)
        return x
    edge_index = jnp.stack([src, dst])
    h = jnp.maximum(_layernorm(x, axis=-1), 0.0)
    x = x + _L0_gnn_ref(h, edge_index, L0_gnn_W_root, L0_gnn_W_rel, L0_gnn_b_rel, L0_gnn_gamma, L0_gnn_beta)
    h = jnp.maximum(_layernorm(x, axis=-1), 0.0)
    x = x + _L1_gnn_ref(h, L1_gnn_W_self0, L1_gnn_W_neigh0, L1_gnn_b0, L1_gnn_W_self1, L1_gnn_W_neigh1, L1_gnn_b1, src, dst)
    h = jnp.maximum(_layernorm(x, axis=-1), 0.0)
    x = x + _L2_gnn_ref(h, edge_index, L2_gnn_W_src, L2_gnn_b_src, L2_gnn_W_dst, L2_gnn_b_dst, L2_gnn_att, L2_gnn_bias_out, L2_gnn_ln_gamma, L2_gnn_ln_beta)
    h = jnp.maximum(_layernorm(x, axis=-1), 0.0)
    x = x + _L3_gnn_ref(h, L3_gnn_w1, L3_gnn_sl1, L3_gnn_b1, L3_gnn_w2, L3_gnn_sl2, L3_gnn_b2, edge_index, edge_type_8)
    return x

_drawn_inputs = setup_inputs


def setup_inputs(seed=0):
    import zlib

    import numpy as np

    out = dict(_drawn_inputs(seed))
    spreads = {'L0_gnn_gamma': (1.0, 0.2),
     'L0_gnn_beta': (0.0, 0.1),
     'L1_gnn_b0': (0.0, 0.1),
     'L1_gnn_b1': (0.0, 0.1),
     'L2_gnn_b_src': (0.0, 0.1),
     'L2_gnn_b_dst': (0.0, 2.0),
     'L2_gnn_bias_out': (0.0, 0.1),
     'L2_gnn_ln_gamma': (1.0, 0.2),
     'L2_gnn_ln_beta': (0.0, 0.1),
     'L3_gnn_b1': (0.0, 0.449),
     'L3_gnn_b2': (0.0, 2.0)}
    factors = {'L0_gnn_b_rel': 64.0, 'L2_gnn_W_dst': 26.407}
    for name, (base, spread) in spreads.items():
        noise = np.random.default_rng([zlib.crc32(name.encode()), seed]).standard_normal(out[name].shape)
        drawn = base * np.exp(spread * noise) if base else spread * noise
        out[name] = jnp.asarray(drawn.astype(out[name].dtype))
    for name, factor in factors.items():
        out[name] = (out[name] * factor).astype(out[name].dtype)
    return out
```

```python
from contextlib import ExitStack

import concourse.bass as bass
from concourse import mybir

F32 = mybir.dt.float32
I32 = mybir.dt.int32
ALU = mybir.AluOpType
ACT = mybir.ActivationFunctionType
AX = mybir.AxisListType
ENG = mybir.EngineType

P = 128
N = 3125
E = 103125
NT = -(-N // P)
NP = NT * P
LAST = N - (NT - 1) * P
ET = -(-E // P)
U = 13
IT = ET // U
GA = 7
W = NP + P
R = 8
HEADS = 8
HD = P // HEADS
NCH = 8
CH = NP // NCH
EPS = 1e-5
BIG = 1e30
LEAD = 4
assert ET % U == 0 and ET * P >= E and CH * 4 <= 2048


class Lane:

    def __init__(self, eng, sem):
        self.eng, self.sem, self.n = eng, sem, 0

    def after(self, *marks):
        if self.n:
            self.eng.wait_ge(self.sem, self.n)
        for sem, n in marks:
            self.eng.wait_ge(sem, n)
        return self.eng

    def need(self, *marks):
        for sem, n in marks:
            self.eng.wait_ge(sem, n)
        return self.eng

    def did(self, ins):
        ins.then_inc(self.sem, 1)
        self.n += 1
        return (self.sem, self.n)

    def now(self):
        return (self.sem, self.n)


class Dma:

    def __init__(self, sem):
        self.sem, self.n = sem, 0

    def did(self, ins):
        ins.then_inc(self.sem, 16)
        self.n += 16
        return (self.sem, self.n)

    def now(self):
        return (self.sem, self.n)


def build(nc, a, out):
    with ExitStack() as ctx:
        def sem(name):
            return ctx.enter_context(nc.semaphore(name))

        def sb(name, shape, dt=F32):
            return ctx.enter_context(nc.sbuf_tensor(name, shape, dt))

        V = Lane(nc.vector, sem("s_dve"))
        A = Lane(nc.scalar, sem("s_act"))
        T = Lane(nc.tensor, sem("s_pe"))
        G = Lane(nc.gpsimd, sem("s_pool"))

        s_tick = sem("s_tick")
        hot_n, mm_n, add_n = sem("s_onehot"), sem("s_product"), sem("s_added")
        tr_n, trc_n, rl_n, lk_n = sem("s_hotT"), sem("s_hotT_copied"), sem("s_relu"), sem("s_leaky")
        lg_n, lgc_n = sem("s_logits"), sem("s_logits_copied")
        s_idx = [sem("s_idxA"), sem("s_idxB")]
        s_row = [sem(f"s_row{k}") for k in range(U)]
        s_win = [sem(f"s_win{k}") for k in range(U)]
        s_save = [sem("s_saveA"), sem("s_saveB")]
        s_lgout = sem("s_logits_out")
        s_lp = [sem("s_probA"), sem("s_probB")]
        s_xe = [sem("s_rowsA"), sem("s_rowsB")]
        msg_n, pb_n = sem("s_msg"), sem("s_pbc")
        cnt = {}
        START = 16
        for s in (s_lgout, *s_save, *s_idx, *s_row, *s_win, *s_lp, *s_xe):
            cnt[s] = 0
        for s in (hot_n, mm_n, add_n, tr_n, trc_n, rl_n, lk_n, lg_n, lgc_n, msg_n, pb_n):
            nc.vector.sem_inc(s, START)
            cnt[s] = START

        X = sb("X", [P, NT, P])
        H = sb("H", [P, NT, P])
        HT = sb("HT", [P, NP])
        B1 = sb("B1", [P, NT, P])
        B1T = B1[:, :, :].rearrange("p t d -> p (t d)")
        invdeg = sb("invdeg", [P, NP])
        acc = sb("acc", [P, 2, W])
        rows = sb("rows", [P, U, P])
        hot = sb("hot", [P, U, P])
        win = sb("win", [P, U, P])
        pbc = sb("pbc", [P, U, P])
        hotT = pbc
        srcs = sb("srcs", [P, ET + U], I32)
        relidx = sb("relidx", [P, ET + U], I32)
        rel = sb("rel", [P, ET + U])
        d0 = sb("d0", [P, ET + U], I32)
        idx = [sb("idxA", [P, GA], I32), sb("idxB", [P, U - GA], I32)]
        iota_i = sb("iota_i", [P, P], I32)
        iota = sb("iota", [P, P])
        ident = sb("ident", [P, P])
        ones = sb("ones", [P, P])
        Wt = {n: sb("w_" + n, [P, P]) for n in ("L0_rel", "L0_root", "L1_s0", "L1_n0", "L1_s1", "L1_n1",
                                                "L2_src", "L2_dst", "L3_sl1", "L3_sl2")}
        wrel = sb("wrel", [P, R, P])
        brow = {n: sb("r_" + n, [1, P]) for n in ("L1_b0", "L1_b1", "L2_b_src", "L2_b_dst", "L3_b1", "L3_b2")}
        bcol = {n: sb("c_" + n, [P, 1]) for n in ("L0_b_rel", "L0_gamma", "L0_beta", "L2_att")}
        bfull = {n: sb("f_" + n, [P, P]) for n in ("L2_bias_out", "L2_ln_gamma", "L2_ln_beta")}
        attm = sb("attm", [P, HEADS])
        st = {n: sb("st_" + n, [P, NT]) for n in ("sum", "mean", "var", "sd", "rstd")}
        bn = {n: sb("bn_" + n, [P, 1]) for n in ("sum", "mean", "ss", "var", "sd", "rstd", "scale")}
        rl = sb("rl", [P, 3, P])
        lk = sb("lk", [P, 3, P])
        lgs = sb("lgs", [P, U * HEADS])
        prob = sb("prob", [P, U, HEADS])
        lg = sb("lg", [P, ET, HEADS])
        fst = sb("fst", [P, ET])
        lst = sb("lst", [P, ET])
        dstr = {n: sb("dstr_" + n, [P, ET], I32) for n in ("own", "prev", "next")}
        car = sb("car", [P, 2 * HEADS])
        cs = sb("cs", [HEADS, 4, P])
        pb = [ctx.enter_context(nc.psum_tensor(f"bank{i}", [P, 512], F32)) for i in range(8)]
        stage = [rows[:, 0:8, :], hot[:, 0:8, :]]

        def dram(name, shape):
            return nc.dram_tensor(name, shape, F32, kind="Internal").ap()

        tabs = [dram(f"tab{i}", [NP, P]) for i in range(3)]
        xs_t, xd_t = dram("xs_t", [NP, P]), dram("xd_t", [W, P])
        rel_t = dram("rel_t", [R * NP, P])
        xs_e = dram("xs_e", [IT, P, U, P])
        lg_e = dram("lg_e", [ET * P, HEADS])
        pr_e = dram("pr_e", [ET * P, HEADS])

        s_in = Dma(sem("s_in"))
        s_x = Dma(sem("s_x"))
        s_par = Dma(sem("s_par"))
        mz = V.did(V.after().memset(X[:, NT - 1, :], 0.0))
        mz2 = V.did(V.after().memset(srcs[:, ET:ET + U], 0))
        V.did(V.after().memset(rel[:, ET:ET + U], 0.0))
        V.did(V.after().memset(relidx[:, ET:ET + U], 0))
        d0z = V.did(V.after().memset(d0[:, ET:ET + U], 0))
        onz = V.did(V.after().memset(ones[:, :], 1.0))
        nc.sync.wait_ge(*mz)
        s_x.did(nc.sync.dma_start(X[:, 0:NT - 1, :], a["x"][0:(NT - 1) * P, :].rearrange("(t p) d -> p t d", p=P)))
        s_x.did(nc.sync.dma_start(X[0:LAST, NT - 1, :], a["x"][(NT - 1) * P:N, :]))
        typ = B1T[:, 0:ET].bitcast(I32)
        dcol = B1T[:, ET:2 * ET].bitcast(I32)
        nc.sync.wait_ge(*d0z)
        s_in.did(nc.sync.dma_start(srcs[:, 0:ET], a["src_col"]))
        s_in.did(nc.sync.dma_start(typ, a["type_col"]))
        s_in.did(nc.sync.dma_start(dcol, a["dst_col"]))
        s_in.did(nc.sync.dma_start(d0[:, 0:ET], a["dst_first"].to_broadcast([P, ET])))
        for n in ("own", "prev", "next"):
            s_par.did(nc.sync.dma_start(dstr[n][:, :], a["dst_" + n]))
        raw = {"L1_s0": a["L1_gnn_W_self0"], "L1_n0": a["L1_gnn_W_neigh0"],
               "L1_s1": a["L1_gnn_W_self1"], "L1_n1": a["L1_gnn_W_neigh1"]}
        wraw = {n: win[:, j, :] for j, n in enumerate(raw)}
        for n, src in raw.items():
            s_par.did(nc.sync.dma_start(wraw[n], src))
        for n, k in (("L0_rel", "L0_gnn_W_rel"), ("L0_root", "L0_gnn_W_root"), ("L2_src", "L2_gnn_W_src"),
                     ("L2_dst", "L2_gnn_W_dst"), ("L3_sl1", "L3_gnn_sl1"), ("L3_sl2", "L3_gnn_sl2")):
            s_par.did(nc.sync.dma_start(Wt[n][:, :], a[k]))
        s_par.did(nc.sync.dma_start(wrel[:, :, :], a["L3_gnn_w1"].rearrange("r d e -> d r e")))
        for n, k in (("L1_b0", "L1_gnn_b0"), ("L1_b1", "L1_gnn_b1"), ("L2_b_src", "L2_gnn_b_src"),
                     ("L2_b_dst", "L2_gnn_b_dst"), ("L3_b1", "L3_gnn_b1"), ("L3_b2", "L3_gnn_b2")):
            s_par.did(nc.sync.dma_start(brow[n][:, :], a[k].rearrange("(a d) -> a d", a=1)))
        for n, k in (("L0_b_rel", "L0_gnn_b_rel"), ("L0_gamma", "L0_gnn_gamma"), ("L0_beta", "L0_gnn_beta")):
            s_par.did(nc.sync.dma_start(bcol[n][:, :], a[k].rearrange("(d a) -> d a", a=1)))
        s_par.did(nc.sync.dma_start(bcol["L2_att"][:, :], a["L2_gnn_att"].rearrange("h (c a) -> (h c) a", a=1)))
        for n, k in (("L2_bias_out", "L2_gnn_bias_out"), ("L2_ln_gamma", "L2_gnn_ln_gamma"),
                     ("L2_ln_beta", "L2_gnn_ln_beta")):
            s_par.did(nc.sync.dma_start(bfull[n][:, :],
                                        a[k].rearrange("(a d) -> a d", a=1).to_broadcast([P, P])))

        G.did(G.after().memset(ident[:, :], 0.0))
        idn = G.did(G.after().affine_select(out=ident[:, :], in_=ident[:, :], compare_op=ALU.not_equal, fill=1.0,
                                            base=0, pattern=[[-1, P]], channel_multiplier=1))
        io = G.did(G.after().iota(iota_i[:, :], pattern=[[1, P]], base=0, channel_multiplier=0))
        G.did(G.after().memset(attm[:, :], 1.0))
        G.did(G.after().affine_select(out=attm[:, :], in_=attm[:, :], compare_op=ALU.is_ge, fill=0.0,
                                      base=0, pattern=[[-HD, HEADS]], channel_multiplier=1))
        am = G.did(G.after().affine_select(out=attm[:, :], in_=attm[:, :], compare_op=ALU.is_ge, fill=0.0,
                                           base=HD - 1, pattern=[[HD, HEADS]], channel_multiplier=-1))
        V.did(V.after(io).tensor_copy(iota[:, :], iota_i[:, :]))
        V.did(V.after(s_in.now()).scalar_tensor_tensor(out=relidx[:, 0:ET], in0=typ, scalar=float(NP),
                                                       in1=srcs[:, 0:ET], op0=ALU.mult, op1=ALU.add))
        tabled = V.did(V.after().tensor_tensor(rel[:, 0:ET], dcol, d0[:, 0:ET], ALU.subtract))
        V.did(V.after(am, s_par.now()).tensor_scalar(attm[:, :], attm[:, :], bcol["L2_att"][:, 0:1], None, ALU.mult))
        V.did(V.after().tensor_tensor(fst[:, :], dstr["own"][:, :], dstr["prev"][:, :], ALU.not_equal))
        V.did(V.after().tensor_tensor(lst[:, :], dstr["own"][:, :], dstr["next"][:, :], ALU.not_equal))
        T.need(idn, s_par.now())
        for j, n in enumerate(raw):
            tw = T.did(nc.tensor.transpose(pb[4][:, j * P:(j + 1) * P], wraw[n], ident[:, :]))
        A.need(tw)
        for j, n in enumerate(raw):
            A.did(nc.scalar.activation(Wt[n][:, :], pb[4][:, j * P:(j + 1) * P], ACT.Copy))
        wt_ready = A.now()

        last_evac = {b: wt_ready for b in (4, 5, 6, 7)}
        rot = [0]

        def groups():
            for g in range(0, NT, 4):
                b = 4 + rot[0] % 4
                rot[0] += 1
                yield b, list(range(g, min(g + 4, NT)))

        def turn(src_tiles, evac, *marks):
            T.need(*marks)
            for b, tiles in groups():
                T.need(last_evac[b])
                for j, t in enumerate(tiles):
                    m = T.did(nc.tensor.transpose(pb[b][:, j * P:(j + 1) * P], src_tiles(t), ident[:, :]))
                last_evac[b] = evac(pb[b][:, 0:len(tiles) * P], tiles, m)

        def product(terms, bias, evac, *marks):
            T.need(*marks)
            for b, tiles in groups():
                T.need(last_evac[b])
                for j, t in enumerate(tiles):
                    o = pb[b][:, j * P:(j + 1) * P]
                    for n, (lhs, rhs) in enumerate(terms):
                        m = nc.tensor.matmul(o, lhs[:, t * P:(t + 1) * P], rhs, start=(n == 0),
                                             stop=(bias is None and n == len(terms) - 1))
                    if bias is not None:
                        m = nc.tensor.matmul(o, ones[0:1, :], bias, start=False, stop=True)
                    m = T.did(m)
                last_evac[b] = evac(pb[b][:, 0:len(tiles) * P], tiles, m)

        def tiles_of(arr, tiles):
            return arr[:, tiles[0]:tiles[-1] + 1, :].rearrange("p t d -> p (t d)")

        def cols_of(arr, tiles):
            return arr[:, tiles[0] * P:(tiles[-1] + 1) * P]

        def to(dst, view, func=ACT.Copy):
            def evac(ps, tiles, m):
                A.need(m)
                return A.did(nc.scalar.activation(view(dst, tiles), ps, func))
            return evac

        def add_to_x(ps, tiles, m):
            V.after(m)
            xv = tiles_of(X, tiles)
            return V.did(nc.vector.tensor_tensor(xv, xv, ps, ALU.add))

        def bc(col):
            return col.unsqueeze(2).to_broadcast([P, NT, P])

        def normalise(src, dst):
            V.did(V.after().tensor_reduce(st["sum"][:, :], src[:, :, :], AX.X, ALU.add))
            V.did(V.after().tensor_scalar(st["mean"][:, :], st["sum"][:, :], 1.0 / P, None, ALU.mult))
            m = V.did(V.after().tensor_tensor(dst[:, :, :], src[:, :, :], bc(st["mean"][:, :]), ALU.subtract))
            m = A.did(A.after(m).activation(B1[:, :, :], dst[:, :, :], ACT.Square))
            V.did(V.after(m).tensor_reduce(st["var"][:, :], B1[:, :, :], AX.X, ALU.add))
            m = V.did(V.after().tensor_scalar(st["var"][:, :], st["var"][:, :], 1.0 / P, EPS, ALU.mult, ALU.add))
            m = A.did(A.after(m).activation(st["sd"][:, :], st["var"][:, :], ACT.Sqrt))
            return V.did(V.after(m).reciprocal(st["rstd"][:, :], st["sd"][:, :]))

        def pre_norm():
            normalise(X, H)
            return V.did(V.after().scalar_tensor_tensor(out=H[:, :, :], in0=H[:, :, :], scalar=0.0,
                                                        in1=bc(st["rstd"][:, :]), op0=ALU.max, op1=ALU.mult))

        s_tab = Dma(sem("s_tab"))

        def write_table(tab, src, mark):
            nc.sync.wait_ge(*mark)
            return s_tab.did(nc.sync.dma_start(tab.rearrange("(t p) d -> p t d", p=P), src[:, :, :]))

        def load_idx(table, g, col, base_wait=None):
            lo = 0 if g == 0 else GA
            return nc.sync.dma_start(idx[g][:, :], table[:, bass.ds(col + lo, idx[g].shape[1])])

        def quiet(eng, s, n):
            eng.wait_ge(s, n)
            eng.sem_inc(s_tick, 1)

        def one_hot(k, col):
            return nc.vector.tensor_scalar(hot[:, k, :], iota[:, :], rel[:, bass.ds(col, 1)], None, ALU.is_equal)

        def first_hots():
            for k in range(LEAD):
                one_hot(k, k).then_inc(hot_n, 1)

        def clear_acc(n):
            ins = V.after().memset(acc[:, 0:n, :], 0.0)
            ins.then_inc(add_n, 1)
            cnt[add_n] += 1

        def first_nodes(eng, tile):
            _, v = nc.values_load_multi_w_load_instructions(d0[0:1, bass.ds(tile, U)], engines=(eng,),
                                                            min_val=0, max_val=N)
            return v

        def add_window(k, i, first, base, mmbase, n):
            nc.vector.wait_ge(mm_n, mmbase + i * U + (k + 1))
            nc.vector.wait_ge(add_n, base + i * U + k)
            av = acc[:, 0:n, bass.ds(first, P)]
            pv = pb[k % 4][:, 0:n * P].rearrange("p (a w) -> p a w", a=n)
            nc.vector.tensor_tensor(av, av, pv, ALU.add).then_inc(add_n, 1)

        def bank_free(k, i, base):
            nc.tensor.wait_ge(add_n, base + i * U + (k - 3 if k else 0))

        def first_idx(table, *marks):
            for m in marks:
                nc.sync.wait_ge(*m)
            nc.sync.wait_ge(mm_n, cnt[mm_n])
            for g in (0, 1):
                nc.sync.wait_ge(s_idx[g], cnt[s_idx[g]])
                load_idx(table, g, 0).then_inc(s_idx[g], 16)
                cnt[s_idx[g]] += 16

        def edge_sum(table, index, ready, with_degree=False):
            n = 2 if with_degree else 1
            clear_acc(n)
            first_idx(index, tabled)
            nc.gpsimd.wait_ge(*ready)
            V.after()
            first_hots()
            base = {s: cnt[s] for s in (hot_n, mm_n, add_n, *s_idx, *s_row)}
            with nc.Fori(0, IT, engines=(ENG.SP, ENG.Pool, ENG.PE, ENG.DVE)) as i:
                for g, last in ((0, GA), (1, U)):
                    quiet(nc.sync, mm_n, base[mm_n] + i * U + last)
                    load_idx(index, g, i * U + U).then_inc(s_idx[g], 16)
                for k in range(U):
                    g = int(k >= GA)
                    if k in (0, GA):
                        quiet(nc.gpsimd, s_idx[g], base[s_idx[g]] + i * 16)
                    c = k - GA * g
                    nc.gpsimd.indirect_dma_start(
                        rows[:, k, :], None, table[:, :],
                        bass.IndirectOffsetOnAxis(ap=idx[g][:, c:c + 1], axis=0)).then_inc(s_row[k], 16)
                first = first_nodes(ENG.DVE, i * U)
                for k in range(U):
                    nc.tensor.wait_ge(hot_n, base[hot_n] + i * U + (k + 1))
                    bank_free(k, i, base[add_n])
                    nc.tensor.wait_ge(s_row[k], base[s_row[k]] + i * 16 + 16)
                    m = nc.tensor.matmul(pb[k % 4][:, 0:P], rows[:, k, :], hot[:, k, :], start=True, stop=True)
                    if with_degree:
                        m = nc.tensor.matmul(pb[k % 4][:, P:2 * P], ones[:, :], hot[:, k, :], start=True, stop=True)
                    m.then_inc(mm_n, 1)
                    one_hot((k + LEAD) % U, i * U + (k + LEAD)).then_inc(hot_n, 1)
                    add_window(k, i, first[k], base[add_n], base[mm_n], n)
            cnt[hot_n] += ET + LEAD
            cnt[mm_n] += ET
            cnt[add_n] += ET
            for s in s_idx + s_row:
                cnt[s] += 16 * IT
            V.need((add_n, cnt[add_n]), (hot_n, cnt[hot_n]))
            return (add_n, cnt[add_n])

        AT = acc[:, 0, 0:NP]
        DG = acc[:, 1, 0:NP]

        V.need(s_x.now())
        h = pre_norm()
        tab = write_table(tabs[0], H, h)
        turn(lambda t: H[:, t, :], to(HT, cols_of), h)
        summed = edge_sum(tabs[0], srcs, tab, with_degree=True)
        V.did(V.after().tensor_scalar(invdeg[:, :], DG, 1.0, None, ALU.max))
        V.did(V.after().reciprocal(invdeg[:, :], invdeg[:, :]))
        for c in range(NCH):
            b = 4 + c % 4
            T.need(last_evac[b], A.now(), summed)
            s = slice(c * CH, (c + 1) * CH)
            nc.tensor.matmul(pb[b][:, 0:CH], Wt["L0_rel"][:, :], AT[:, s], start=True, stop=False)
            m = T.did(nc.tensor.matmul(pb[b][:, 0:CH], Wt["L0_root"][:, :], HT[:, s], start=False, stop=True))
            A.need(m)
            last_evac[b] = A.did(nc.scalar.activation(B1T[:, s], pb[b][:, 0:CH], ACT.Identity,
                                                      bias=bcol["L0_b_rel"][:, 0:1]))
        uT = B1T[:, 0:N]
        V.did(V.after(A.now()).tensor_reduce(bn["sum"][:, :], uT, AX.X, ALU.add))
        V.did(V.after().tensor_scalar(bn["mean"][:, :], bn["sum"][:, :], 1.0 / N, None, ALU.mult))
        m = V.did(V.after().tensor_scalar(B1T[:, :], B1T[:, :], bn["mean"][:, 0:1], None, ALU.subtract))
        m = A.did(A.after(m, T.now()).activation(HT[:, 0:N], uT, ACT.Square))
        V.did(V.after(m).tensor_reduce(bn["ss"][:, :], HT[:, 0:N], AX.X, ALU.add))
        m = V.did(V.after().tensor_scalar(bn["var"][:, :], bn["ss"][:, :], 1.0 / N, EPS, ALU.mult, ALU.add))
        m = A.did(A.after(m).activation(bn["sd"][:, :], bn["var"][:, :], ACT.Sqrt))
        V.did(V.after(m).reciprocal(bn["rstd"][:, :], bn["sd"][:, :]))
        m = V.did(V.after().tensor_tensor(bn["scale"][:, :], bn["rstd"][:, :], bcol["L0_gamma"][:, :], ALU.mult))
        m = A.did(A.after(m).activation(HT[:, :], B1T[:, :], ACT.Relu, bias=bcol["L0_beta"][:, 0:1],
                                        scale=bn["scale"][:, 0:1]))
        turn(lambda t: HT[:, t * P:(t + 1) * P], add_to_x, m)

        h = pre_norm()
        A.need(T.now())
        tab = write_table(tabs[1], H, h)
        turn(lambda t: H[:, t, :], to(HT, cols_of), h)
        edge_sum(tabs[1], srcs, tab)
        m = V.did(V.after().tensor_tensor(AT, AT, invdeg[:, :], ALU.mult))
        nc.scalar.wait_ge(*tab)
        product([(HT, Wt["L1_s0"][:, :]), (AT, Wt["L1_n0"][:, :])], brow["L1_b0"][:, :],
                to(H, tiles_of, ACT.Relu), m, A.now())
        tab = write_table(tabs[2], H, A.now())
        A.need(T.now())
        turn(lambda t: H[:, t, :], to(HT, cols_of), A.now())
        V.need(T.now())
        edge_sum(tabs[2], srcs, tab)
        m = V.did(V.after().tensor_tensor(AT, AT, invdeg[:, :], ALU.mult))
        product([(HT, Wt["L1_s1"][:, :]), (AT, Wt["L1_n1"][:, :])], brow["L1_b1"][:, :], add_to_x, m, A.now())

        V.need(tab)
        h = pre_norm()
        A.need(T.now())
        turn(lambda t: H[:, t, :], to(HT, cols_of), h)
        product([(HT, Wt["L2_src"][:, :])], brow["L2_b_src"][:, :], to(B1, tiles_of), A.now(), h)
        m = A.now()
        t1 = write_table(xs_t, B1, m)
        A.need(t1)
        product([(HT, Wt["L2_dst"][:, :])], brow["L2_b_dst"][:, :], to(B1, tiles_of), m)
        t2 = write_table(xd_t[0:NP, :], B1, A.now())
        for s, lo, hi in ((s_save[0], 0, 64), (s_save[1], 64, 96), (s_lgout, 96, P)):
            nc.sync.dma_start(xd_t[NP + lo:NP + hi, :], ones[lo:hi, :]).then_inc(s, 16)
            cnt[s] += 16
            nc.sync.wait_ge(s, cnt[s])
        tab = s_tab.now()

        TS = [k % 2 for k in range(U - 1)] + [2]
        TB = [(0, 1, 5)[s] for s in TS]
        EB = [(2, 3, 6)[s] for s in TS]
        def load_window(k, tile):
            first = nc.sync.value_load(d0[0:1, bass.ds(tile, 1)], min_val=0, max_val=N)
            return nc.sync.dma_start(win[:, k, :], xd_t[bass.ds(first, P), :])

        first_idx(srcs, tab)
        nc.gpsimd.wait_ge(*tab)
        nc.tensor.wait_ge(*A.now())
        with nc.allow_non_contiguous_dma(reason="window rows"):
            for k in range(U):
                load_window(k, k).then_inc(s_win[k], 16)
                cnt[s_win[k]] += 16
        V.after()
        first_hots()
        base = dict(cnt)
        A.after()

        def turn_hot(k):
            nc.tensor.transpose(pb[TB[k]][:, 0:P], hot[:, k, :], ident[:, :]).then_inc(tr_n, 1)

        def copy_hot(k):
            nc.scalar.activation(hotT[:, k, :], pb[TB[k]][:, 0:P], ACT.Copy).then_inc(trc_n, 1)

        for k in (0, 1):
            nc.tensor.wait_ge(hot_n, base[hot_n] + k + 1)
            turn_hot(k)
        nc.scalar.wait_ge(tr_n, base[tr_n] + 1)
        copy_hot(0)
        with nc.Fori(0, IT, engines=(ENG.SP, ENG.Pool, ENG.PE, ENG.DVE, ENG.Activation)) as i:
            n0 = i * U
            first = first_nodes(ENG.SP, n0 + U)
            for k in range(U):
                quiet(nc.sync, mm_n, base[mm_n] + n0 + (k + 1))
                nc.sync.dma_start(win[:, k, :], xd_t[bass.ds(first[k], P), :]).then_inc(s_win[k], 16)
                if k in (GA - 1, U - 1):
                    g = int(k >= GA)
                    lo, hi = (0, GA) if g == 0 else (GA, U)
                    nc.sync.dma_start(xs_e[bass.ds(i, 1), :, lo:hi, :].rearrange("i p k d -> (i p) (k d)"),
                                      rows[:, lo:hi, :].rearrange("p k d -> p (k d)")).then_inc(s_save[g], 16)
                    load_idx(srcs, g, n0 + U).then_inc(s_idx[g], 16)
            quiet(nc.sync, lgc_n, base[lgc_n] + i + 1)
            nc.sync.dma_start(lg_e.rearrange("(t p) h -> p t h", p=P)[:, bass.ds(n0, U), :],
                              lgs[:, :].rearrange("p (k h) -> p k h", k=U)).then_inc(s_lgout, 16)
            for k in range(U):
                g = int(k >= GA)
                if k in (0, GA):
                    quiet(nc.gpsimd, s_idx[g], base[s_idx[g]] + i * 16)
                    quiet(nc.gpsimd, s_save[g], base[s_save[g]] + i * 16)
                c = k - GA * g
                nc.gpsimd.indirect_dma_start(
                    rows[:, k, :], None, xs_t[:, :],
                    bass.IndirectOffsetOnAxis(ap=idx[g][:, c:c + 1], axis=0)).then_inc(s_row[k], 16)
            def logits(j):
                nc.tensor.wait_ge(lk_n, base[lk_n] + n0 + (j + 1))
                nc.tensor.matmul(pb[4][:, j * HEADS:(j + 1) * HEADS], lk[:, TS[j], :], attm[:, :],
                                 start=True, stop=True).then_inc(lg_n, 1)

            for k in range(U):
                nc.tensor.wait_ge(hot_n, base[hot_n] + n0 + (k + 3))
                nc.tensor.wait_ge(trc_n, base[trc_n] + n0 + (k + 1))
                turn_hot((k + 2) % U)
                nc.scalar.wait_ge(tr_n, base[tr_n] + n0 + (k + 2))
                copy_hot((k + 1) % U)
                nc.tensor.wait_ge(s_win[k], base[s_win[k]] + i * 16)
                nc.tensor.wait_ge(lk_n, base[lk_n] + n0 + (k - 1))
                nc.tensor.matmul(pb[EB[k]][:, 0:P], win[:, k, :], hotT[:, k, :], start=True, stop=False)
                nc.tensor.wait_ge(s_row[k], base[s_row[k]] + i * 16 + 16)
                nc.tensor.matmul(pb[EB[k]][:, 0:P], rows[:, k, :], ident[:, :], start=False,
                                 stop=True).then_inc(mm_n, 1)
                nc.scalar.wait_ge(mm_n, base[mm_n] + n0 + (k + 1))
                nc.scalar.wait_ge(lk_n, base[lk_n] + n0 + (k - 1))
                nc.scalar.activation(rl[:, TS[k], :], pb[EB[k]][:, 0:P], ACT.Relu, scale=0.8).then_inc(rl_n, 1)
                nc.vector.wait_ge(tr_n, base[tr_n] + n0 + (k + 1))
                one_hot((k + LEAD) % U, n0 + (k + LEAD)).then_inc(hot_n, 1)
                nc.vector.wait_ge(rl_n, base[rl_n] + n0 + (k + 1))
                nc.vector.wait_ge(lg_n, base[lg_n] + n0 + (k - 1 if k > 1 else 0))
                nc.vector.scalar_tensor_tensor(out=lk[:, TS[k], :], in0=pb[EB[k]][:, 0:P], scalar=0.2,
                                               in1=rl[:, TS[k], :], op0=ALU.mult, op1=ALU.add).then_inc(lk_n, 1)
                if k == 2:
                    nc.tensor.wait_ge(lgc_n, base[lgc_n] + i)
                if k > 1:
                    logits(k - 2)
            logits(U - 2)
            logits(U - 1)
            nc.scalar.wait_ge(lg_n, base[lg_n] + n0 + U)
            nc.scalar.wait_ge(s_lgout, base[s_lgout] + i * 16)
            nc.scalar.activation(lgs[:, :], pb[4][:, 0:U * HEADS], ACT.Copy).then_inc(lgc_n, 1)
        for s in (mm_n, trc_n, rl_n, lk_n, lg_n):
            cnt[s] += ET
        cnt[hot_n] += ET + LEAD
        cnt[tr_n] += ET + 2
        cnt[trc_n] += 1
        cnt[lgc_n] += IT
        for s in (*s_idx, *s_row, *s_win, *s_save, s_lgout):
            cnt[s] += 16 * IT

        s_b = Dma(sem("s_softmax"))
        nc.sync.wait_ge(s_lgout, cnt[s_lgout])
        lgin = s_b.did(nc.sync.dma_start(lg[:, :, :], lg_e.rearrange("(p t) h -> p t h", p=P)))
        sm = acc[:, :, :].rearrange("p a w -> p (a w)")[:, 0:ET * HEADS].rearrange("p (t h) -> p t h", h=HEADS)
        fl = [B1T[:, 0:ET], B1T[:, ET:2 * ET]]
        tmp = B1T[:, 2 * ET:2 * ET + 1]

        def scan(v, f, n, heads, t, backward):
            def run(lo, step, num):
                if backward:
                    first = n - 1 - lo
                    return bass.ds(first - step * (num - 1), num, step=step) if step > 1 else slice(first - num + 1, first + 1)
                return bass.ds(lo, num, step=step) if step > 1 else slice(lo, lo + num)

            def combine(left, right, step, num):
                ls, rs = run(left, step, num), run(right, step, num)
                if heads:
                    fr = f[:, rs].unsqueeze(2).to_broadcast([v.shape[0], num, HEADS])
                    vl, vr, tt = v[:, ls, :], v[:, rs, :], t[:, 0:num, :]
                else:
                    fr, vl, vr, tt = f[:, rs], v[:, ls], v[:, rs], t[:, 0:num]
                V.did(V.after().scalar_tensor_tensor(out=tt, in0=fr, scalar=-BIG, in1=vl, op0=ALU.mult, op1=ALU.add))
                V.did(V.after().tensor_tensor(vr, vr, tt, ALU.max))
                V.did(V.after().tensor_tensor(f[:, rs], f[:, rs], f[:, ls], ALU.max))

            s = 1
            while 2 * s <= n:
                combine(s - 1, 2 * s - 1, 2 * s, n // (2 * s))
                s *= 2
            while s >= 1:
                num = (n - 3 * s) // (2 * s) + 1 if n >= 3 * s else 0
                if num > 0:
                    combine(2 * s - 1, 3 * s - 1, 2 * s, num)
                s //= 2

        def carry(v, f, backward):
            e = ET - 1 if not backward else 0
            V.did(V.after().tensor_copy(car[:, 0:HEADS], v[:, e, :]))
            m = V.did(V.after().tensor_copy(car[:, HEADS:2 * HEADS], f[:, e:e + 1].to_broadcast([P, HEADS])))
            T.need(m, idn)
            nc.tensor.transpose(pb[5][0:HEADS, 0:P], car[:, 0:HEADS], ident[:, :])
            m = T.did(nc.tensor.transpose(pb[5][0:HEADS, P:2 * P], car[:, HEADS:2 * HEADS], ident[:, :]))
            V.did(V.after(m).tensor_copy(cs[:, 0:2, :], pb[5][0:HEADS, 0:2 * P].rearrange("h (a p) -> h a p", a=2)))
            scan(cs[:, 0, :], cs[:, 1, :], P, False, cs[:, 2, :], backward)
            V.did(V.after().memset(cs[:, 3, :], -BIG))
            if backward:
                m = V.did(V.after().tensor_copy(cs[:, 3, 0:P - 1], cs[:, 0, 1:P]))
            else:
                m = V.did(V.after().tensor_copy(cs[:, 3, 1:P], cs[:, 0, 0:P - 1]))
            T.need(m)
            m = T.did(nc.tensor.transpose(pb[5][:, 0:HEADS], cs[:, 3, :], ident[0:HEADS, 0:HEADS]))
            V.did(V.after(m).tensor_copy(car[:, 0:HEADS], pb[5][:, 0:HEADS]))
            cb = car[:, 0:HEADS].unsqueeze(1).to_broadcast([P, ET, HEADS])
            V.did(V.after().scalar_tensor_tensor(out=sm, in0=f[:, 0:ET].unsqueeze(2).to_broadcast([P, ET, HEADS]),
                                                 scalar=-BIG, in1=cb, op0=ALU.mult, op1=ALU.add))
            V.did(V.after().tensor_tensor(v, v, sm, ALU.max))

        V.need(t2)
        V.did(V.after().tensor_copy(fl[0], fst[:, :]))
        V.did(V.after(lgin).tensor_copy(fl[1], lst[:, :]))
        lv = lg[:, :, :]
        scan(lv, fl[0], ET, True, sm, False)
        carry(lv, fl[0], False)
        scan(lv, fl[1], ET, True, sm, True)
        carry(lv, fl[1], True)
        nc.sync.wait_ge(*V.now())
        again = s_b.did(nc.sync.dma_start(sm, lg_e.rearrange("(p t) h -> p t h", p=P)))
        m = V.did(V.after(again).tensor_tensor(lv, sm, lv, ALU.subtract))
        m = A.did(A.after(m).activation(lv, lv, ACT.Exp))
        m = V.did(V.after(m).scalar_tensor_tensor(out=lv, in0=lst[:, :].unsqueeze(2).to_broadcast([P, ET, HEADS]),
                                                  scalar=1.0, in1=lv, op0=ALU.add, op1=ALU.mult))
        nc.sync.wait_ge(*m)
        s_b.did(nc.sync.dma_start(pr_e.rearrange("(p t) h -> p t h", p=P), lv))
        probs = s_b.now()

        clear_acc(2)
        nc.sync.wait_ge(*probs)
        for g in (0, 1):
            nc.sync.wait_ge(s_save[g], cnt[s_save[g]])
        nc.sync.wait_ge(lk_n, cnt[lk_n])
        nc.sync.wait_ge(mm_n, cnt[mm_n])
        for k in range(U):
            nc.gpsimd.wait_ge(s_win[k], cnt[s_win[k]])
        span = ((0, GA), (GA, U))

        def load_edges(g, it):
            lo, hi = span[g]
            nc.sync.dma_start(rows[:, lo:hi, :].rearrange("p k d -> p (k d)"),
                              xs_e[bass.ds(it, 1), :, lo:hi, :].rearrange("i p k d -> (i p) (k d)")
                              ).then_inc(s_xe[g], 16)
            nc.sync.dma_start(prob[:, lo:hi, :],
                              pr_e.rearrange("(t p) h -> p t h", p=P)[:, bass.ds(it * U + lo, hi - lo), :]
                              ).then_inc(s_lp[g], 16)

        for g in (0, 1):
            load_edges(g, 0)
            cnt[s_xe[g]] += 16
            cnt[s_lp[g]] += 16
        V.after()
        first_hots()
        base = dict(cnt)

        def attend(i, load_next):
            for g in (0, 1):
                lo, hi = span[g]
                w = hi - lo
                quiet(nc.gpsimd, s_xe[g], base[s_xe[g]] + i * 16)
                quiet(nc.gpsimd, s_lp[g], base[s_lp[g]] + i * 16)
                quiet(nc.gpsimd, mm_n, base[mm_n] + i * U + (hi - U))
                pg = prob[:, lo:hi, :].rearrange("p k h -> p (k h)").unsqueeze(2).to_broadcast([P, w * HEADS, HD])
                nc.gpsimd.tensor_tensor(win[:, lo:hi, :].rearrange("p k (h c) -> p (k h) c", c=HD),
                                        rows[:, lo:hi, :].rearrange("p k (h c) -> p (k h) c", c=HD),
                                        pg, ALU.mult).then_inc(msg_n, 1)
                nc.scalar.wait_ge(s_lp[g], base[s_lp[g]] + i * 16)
                nc.scalar.wait_ge(mm_n, base[mm_n] + i * U + (hi - U))
                nc.scalar.activation(pbc[:, lo:hi, :].rearrange("p k (h c) -> p (k h) c", c=HD), pg,
                                     ACT.Copy).then_inc(pb_n, 1)
                if load_next:
                    quiet(nc.sync, msg_n, base[msg_n] + i * 2 + (g + 1))
                    quiet(nc.sync, pb_n, base[pb_n] + i * 2 + (g + 1))
                    load_edges(g, i + 1)
            first = first_nodes(ENG.DVE, i * U)
            for k in range(U):
                g = int(k >= GA)
                nc.tensor.wait_ge(hot_n, base[hot_n] + i * U + (k + 1))
                bank_free(k, i, base[add_n])
                if k in (0, GA):
                    nc.tensor.wait_ge(msg_n, base[msg_n] + i * 2 + (g + 1))
                    nc.tensor.wait_ge(pb_n, base[pb_n] + i * 2 + (g + 1))
                nc.tensor.matmul(pb[k % 4][:, 0:P], win[:, k, :], hot[:, k, :], start=True, stop=True)
                nc.tensor.matmul(pb[k % 4][:, P:2 * P], pbc[:, k, :], hot[:, k, :], start=True,
                                 stop=True).then_inc(mm_n, 1)
                one_hot((k + LEAD) % U, i * U + (k + LEAD)).then_inc(hot_n, 1)
                add_window(k, i, first[k], base[add_n], base[mm_n], 2)

        with nc.Fori(0, IT - 1, engines=(ENG.SP, ENG.Pool, ENG.PE, ENG.DVE, ENG.Activation)) as i:
            attend(i, True)
        attend(IT - 1, False)
        cnt[hot_n] += ET + LEAD
        cnt[mm_n] += ET
        cnt[add_n] += ET
        cnt[msg_n] += 2 * IT
        cnt[pb_n] += 2 * IT
        for g in (0, 1):
            cnt[s_xe[g]] += 16 * (IT - 1)
            cnt[s_lp[g]] += 16 * (IT - 1)
        V.need((add_n, cnt[add_n]), (hot_n, cnt[hot_n]), (pb_n, cnt[pb_n]), (msg_n, cnt[msg_n]))
        V.did(V.after().tensor_scalar(DG, DG, 1e-30, None, ALU.max))
        V.did(V.after().reciprocal(DG, DG))
        m = V.did(V.after().tensor_tensor(HT[:, :], AT, DG, ALU.mult))

        def add_to_h(ps, tiles, m):
            V.after(m)
            hv = tiles_of(H, tiles)
            return V.did(nc.vector.tensor_tensor(hv, hv, ps, ALU.add))

        turn(lambda t: HT[:, t * P:(t + 1) * P], add_to_h, m)
        def bcr(n):
            return bfull[n][:, :].unsqueeze(1).to_broadcast([P, NT, P])

        V.did(V.after().tensor_tensor(H[:, :, :], H[:, :, :], bcr("L2_bias_out"), ALU.add))
        normalise(H, H)
        V.did(V.after().tensor_tensor(H[:, :, :], H[:, :, :], bc(st["rstd"][:, :]), ALU.mult))
        V.did(V.after().tensor_tensor(H[:, :, :], H[:, :, :], bcr("L2_ln_gamma"), ALU.mult))
        m = V.did(V.after().tensor_tensor(H[:, :, :], H[:, :, :], bcr("L2_ln_beta"), ALU.add))
        m = A.did(A.after(m).activation(H[:, :, :], H[:, :, :], ACT.Gelu))
        V.did(V.after(m).tensor_tensor(X[:, :, :], X[:, :, :], H[:, :, :], ALU.add))

        h = pre_norm()
        A.need(T.now())
        turn(lambda t: H[:, t, :], to(HT, cols_of), h)
        s_rt = [Dma(sem("s_rtabA")), Dma(sem("s_rtabB"))]
        wload = s_par.now()

        def relation_tables(*marks):
            T.need(*marks)
            for t in range(NT):
                sl = t % 2
                for half in (0, 1):
                    b = 4 + 2 * sl + half
                    T.need(last_evac[b])
                    m = T.did(nc.tensor.matmul(pb[b][:, :], HT[:, t * P:(t + 1) * P],
                                               wrel[:, 4 * half:4 * half + 4, :].rearrange("d r e -> d (r e)"),
                                               start=True, stop=True))
                    dst = stage[sl][:, 4 * half:4 * half + 4, :].rearrange("p r e -> p (r e)")
                    if half == 0:
                        A.need(m, s_rt[sl].now())
                        last_evac[b] = ma = A.did(nc.scalar.activation(dst, pb[b][:, :], ACT.Copy))
                    else:
                        V.need(m, s_rt[sl].now())
                        last_evac[b] = mv = V.did(nc.vector.tensor_copy(dst, pb[b][:, :]))
                nc.sync.wait_ge(*ma)
                nc.sync.wait_ge(*mv)
                s_rt[sl].did(nc.sync.dma_start(
                    rel_t.rearrange("(r t p) e -> t p r e", r=R, p=P)[t], stage[sl]))
            nc.gpsimd.wait_ge(*s_rt[0].now())
            V.need(s_rt[0].now(), s_rt[1].now())
            return s_rt[1].now()

        V.need((hot_n, cnt[hot_n]))
        ready = relation_tables(A.now(), s_par.now())
        wused = T.now()
        nc.sync.wait_ge(*wused)
        w2 = s_par.did(nc.sync.dma_start(wrel[:, :, :], a["L3_gnn_w2"].rearrange("r d e -> d r e")))
        V.need(s_rt[1].now())
        m = edge_sum(rel_t, relidx, ready)
        product([(HT, Wt["L3_sl1"][:, :]), (AT, ident[:, :])], brow["L3_b1"][:, :],
                to(H, tiles_of, ACT.Relu), m, A.now())
        A.need(T.now())
        turn(lambda t: H[:, t, :], to(HT, cols_of), A.now())
        A.need((mm_n, cnt[mm_n]))
        V.need((mm_n, cnt[mm_n]), T.now())
        ready = relation_tables(A.now(), w2)
        m = edge_sum(rel_t, relidx, ready)

        def relu_to_x(ps, tiles, m):
            V.after(m)
            xv = tiles_of(X, tiles)
            return V.did(nc.vector.scalar_tensor_tensor(out=xv, in0=ps, scalar=0.0, in1=xv, op0=ALU.max, op1=ALU.add))

        product([(HT, Wt["L3_sl2"][:, :]), (AT, ident[:, :])], brow["L3_b2"][:, :], relu_to_x, m, A.now())
        nc.sync.wait_ge(*V.now())
        s_out = Dma(sem("s_out"))
        s_out.did(nc.sync.dma_start(out[0:(NT - 1) * P, :].rearrange("(t p) d -> p t d", p=P), X[:, 0:NT - 1, :]))
        s_out.did(nc.sync.dma_start(out[(NT - 1) * P:N, :], X[0:LAST, NT - 1, :]))
        nc.sync.wait_ge(*s_out.now())
        for g in (0, 1):
            nc.sync.wait_ge(s_idx[g], cnt[s_idx[g]])


def kernel(**inputs):
    import numpy as np
    import concourse.bacc as bacc
    from concourse.bass_utils import run_bass_kernel_spmd

    pad = ET * P - E
    src, dst, typ = (np.ascontiguousarray(inputs[n]) for n in ("src", "dst", "edge_type_8"))
    src = np.concatenate([src, np.zeros(pad, src.dtype)])
    typ = np.concatenate([typ, np.zeros(pad, typ.dtype)])
    dst = np.concatenate([dst, np.full(pad, N, dst.dtype)])
    end = np.full(1, -1, dst.dtype)
    arrays = {
        "src_col": src.reshape(ET, P).T, "type_col": typ.reshape(ET, P).T, "dst_col": dst.reshape(ET, P).T,
        "dst_first": dst[::P][None, :], "dst_own": dst.reshape(P, ET),
        "dst_prev": np.concatenate([end, dst[:-1]]).reshape(P, ET),
        "dst_next": np.concatenate([dst[1:], end]).reshape(P, ET),
    }
    for n, v in inputs.items():
        if n not in ("src", "dst", "edge_type_8"):
            arrays[n] = v
    arrays = {n: np.ascontiguousarray(v) for n, v in arrays.items()}
    nc = bacc.Bacc("TRN2", target_bir_lowering=False, num_devices=1)
    aps = {n: nc.dram_tensor("in_" + n, v.shape, mybir.dt.from_np(v.dtype), kind="ExternalInput").ap()
           for n, v in arrays.items()}
    out = nc.dram_tensor("out", (N, P), F32, kind="ExternalOutput").ap()
    build(nc, aps, out)
    r = run_bass_kernel_spmd(nc, [{"in_" + n: v for n, v in arrays.items()}], core_ids=[0])
    return r.results[0]["out"]
```

```python
from contextlib import ExitStack

import concourse.bass as bass
from concourse import mybir

F32 = mybir.dt.float32
I32 = mybir.dt.int32
ALU = mybir.AluOpType
ACT = mybir.ActivationFunctionType
AX = mybir.AxisListType
ENG = mybir.EngineType

P = 128
N = 3125
E = 103125
NT = -(-N // P)
NP = NT * P
LAST = N - (NT - 1) * P
ET = -(-E // P)
U = 13
IT = ET // U
GA = 7
PAIR = 4096
W = PAIR + P
R = 8
HEADS = 8
HD = P // HEADS
NCH = 8
CH = NP // NCH
EPS = 1e-5
BIG = 1e30
LEAD = 4
assert N < PAIR and PAIR * (N + 1) < 1 << 24
assert ET % U == 0 and ET * P >= E and CH * 4 <= 2048


class Lane:

    def __init__(self, eng, sem):
        self.eng, self.sem, self.n = eng, sem, 0

    def after(self, *marks):
        if self.n:
            self.eng.wait_ge(self.sem, self.n)
        for sem, n in marks:
            self.eng.wait_ge(sem, n)
        return self.eng

    def need(self, *marks):
        for sem, n in marks:
            self.eng.wait_ge(sem, n)
        return self.eng

    def did(self, ins):
        ins.then_inc(self.sem, 1)
        self.n += 1
        return (self.sem, self.n)

    def now(self):
        return (self.sem, self.n)


class Dma:

    def __init__(self, sem):
        self.sem, self.n = sem, 0

    def did(self, ins):
        ins.then_inc(self.sem, 16)
        self.n += 16
        return (self.sem, self.n)

    def now(self):
        return (self.sem, self.n)


def build(nc, a, out):
    with ExitStack() as ctx:
        def sem(name):
            return ctx.enter_context(nc.semaphore(name))

        def sb(name, shape, dt=F32):
            return ctx.enter_context(nc.sbuf_tensor(name, shape, dt))

        V = Lane(nc.vector, sem("s_dve"))
        A = Lane(nc.scalar, sem("s_act"))
        T = Lane(nc.tensor, sem("s_pe"))
        G = Lane(nc.gpsimd, sem("s_pool"))

        s_tick = sem("s_tick")
        hot_n, mm_n, add_n = sem("s_onehot"), sem("s_product"), sem("s_added")
        tr_n, trc_n, rl_n, lk_n = sem("s_hotT"), sem("s_hotT_copied"), sem("s_relu"), sem("s_leaky")
        lg_n, lgc_n, sq_n = sem("s_logits"), sem("s_logits_copied"), sem("s_squared")
        s_idx = [sem("s_idxA"), sem("s_idxB")]
        s_row = [sem(f"s_row{k}") for k in range(U)]
        s_win = [sem(f"s_win{k}") for k in range(U)]
        s_save = [sem("s_saveA"), sem("s_saveB")]
        s_lgout = sem("s_logits_out")
        s_lp = [sem("s_probA"), sem("s_probB")]
        s_xe = [sem("s_rowsA"), sem("s_rowsB")]
        msg_n, pb_n = sem("s_msg"), sem("s_pbc")
        cnt = {}
        START = 16
        for s in (s_lgout, *s_save, *s_idx, *s_row, *s_win, *s_lp, *s_xe):
            cnt[s] = 0
        for s in (hot_n, mm_n, add_n, tr_n, trc_n, rl_n, lk_n, lg_n, lgc_n, sq_n, msg_n, pb_n):
            nc.vector.sem_inc(s, START)
            cnt[s] = START

        X = sb("X", [P, NT, P])
        H = sb("H", [P, NT, P])
        HT = sb("HT", [P, NP])
        B1 = sb("B1", [P, NT, P])
        B1T = B1[:, :, :].rearrange("p t d -> p (t d)")
        invdeg = sb("invdeg", [P, NP])
        acc = sb("acc", [P, 2, W])
        rows = sb("rows", [P, U, P])
        hot = sb("hot", [P, U, P])
        win = sb("win", [P, U, P])
        pbc = sb("pbc", [P, U, P])
        hotT = pbc
        srcs = sb("srcs", [P, ET + U], I32)
        relidx = sb("relidx", [P, ET + U], I32)
        rel = sb("rel", [P, ET + U])
        d0 = sb("d0", [P, ET + U + 1], I32)
        d0two = sb("d0two", [1, ET + U], I32)
        idx = [sb("idxA", [P, GA], I32), sb("idxB", [P, U - GA], I32)]
        iota_i = sb("iota_i", [P, P], I32)
        iota = sb("iota", [P, P])
        ident = sb("ident", [P, P])
        ones = sb("ones", [P, P])
        Wt = {n: sb("w_" + n, [P, P]) for n in ("L0_rel", "L0_root", "L1_s0", "L1_n0", "L1_s1", "L1_n1",
                                                "L3_sl1", "L3_sl2")}
        wrel = sb("wrel", [P, R, P])
        bcol = {n: sb("c_" + n, [P, 1]) for n in ("L0_b_rel", "L0_gamma", "L0_beta", "L2_att")}
        bfull = {n: sb("f_" + n, [P, P]) for n in ("L1_b0", "L1_b1", "L3_b1", "L3_b2", "L2_bias_out",
                                                   "L2_ln_gamma", "L2_ln_beta")}
        w_sd = sb("w_sd", [P, 2 * P])
        b_sd = sb("b_sd", [P, 2 * P])
        attm = sb("attm", [P, HEADS])
        st = {n: sb("st_" + n, [P, NT]) for n in ("sum", "mean", "var", "sd", "rstd")}
        st["sd8"] = sb("st_rden", [P, NT, HEADS])
        bn = {n: sb("bn_" + n, [P, 1]) for n in ("sum", "mean", "ss", "var", "sd", "rstd", "scale")}
        rl = sb("rl", [P, 3, P])
        lk = sb("lk", [P, 3, P])
        lgs = sb("lgs", [P, U * HEADS])
        prob = sb("prob", [P, U, HEADS])
        lg = sb("lg", [P, ET, HEADS])
        fst = sb("fst", [P, ET])
        lst = sb("lst", [P, ET])
        dstr = {n: sb("dstr_" + n, [P, ET], I32) for n in ("own", "prev", "next")}
        car = sb("car", [P, 2 * HEADS])
        cs = sb("cs", [HEADS, 4, P])
        pb = [ctx.enter_context(nc.psum_tensor(f"bank{i}", [P, 512], F32)) for i in range(8)]
        stage = [rows[:, 0:8, :], hot[:, 0:8, :]]

        def dram(name, shape):
            return nc.dram_tensor(name, shape, F32, kind="Internal").ap()

        tabs = [dram(f"tab{i}", [NP, P]) for i in range(3)]
        xs_t, xd_t = dram("xs_t", [NP, P]), dram("xd_t", [W, P])
        rel_t = dram("rel_t", [R * NP, P])
        xs_e = dram("xs_e", [IT, P, U, P])
        lg_e = dram("lg_e", [ET * P, HEADS])
        pr_e = dram("pr_e", [ET * P, HEADS])

        s_in = Dma(sem("s_in"))
        s_x = Dma(sem("s_x"))
        s_par = Dma(sem("s_par"))
        mz = V.did(V.after().memset(X[:, NT - 1, :], 0.0))
        mz2 = V.did(V.after().memset(srcs[:, ET:ET + U], 0))
        V.did(V.after().memset(rel[:, ET:ET + U], 0.0))
        V.did(V.after().memset(relidx[:, ET:ET + U], 0))
        d0z = V.did(V.after().memset(d0[:, ET:ET + U + 1], 0))
        onz = V.did(V.after().memset(ones[:, :], 1.0))
        nc.sync.wait_ge(*mz)
        s_x.did(nc.sync.dma_start(X[:, 0:NT - 1, :], a["x"][0:(NT - 1) * P, :].rearrange("(t p) d -> p t d", p=P)))
        s_x.did(nc.sync.dma_start(X[0:LAST, NT - 1, :], a["x"][(NT - 1) * P:N, :]))
        typ = B1T[:, 0:ET].bitcast(I32)
        dcol = B1T[:, ET:2 * ET].bitcast(I32)
        nc.sync.wait_ge(*d0z)
        s_in.did(nc.sync.dma_start(srcs[:, 0:ET], a["src_col"]))
        s_in.did(nc.sync.dma_start(typ, a["type_col"]))
        s_in.did(nc.sync.dma_start(dcol, a["dst_col"]))
        s_in.did(nc.sync.dma_start(d0[:, 0:ET], a["dst_first"].to_broadcast([P, ET])))
        for n in ("own", "prev", "next"):
            s_par.did(nc.sync.dma_start(dstr[n][:, :], a["dst_" + n]))
        raw = {"L1_s0": a["L1_gnn_W_self0"], "L1_n0": a["L1_gnn_W_neigh0"],
               "L1_s1": a["L1_gnn_W_self1"], "L1_n1": a["L1_gnn_W_neigh1"]}
        wraw = {n: win[:, j, :] for j, n in enumerate(raw)}
        for n, src in raw.items():
            s_par.did(nc.sync.dma_start(wraw[n], src))
        for dst, k in ((Wt["L0_rel"], "L0_gnn_W_rel"), (Wt["L0_root"], "L0_gnn_W_root"),
                       (w_sd[:, 0:P], "L2_gnn_W_src"), (w_sd[:, P:2 * P], "L2_gnn_W_dst"),
                       (Wt["L3_sl1"], "L3_gnn_sl1"), (Wt["L3_sl2"], "L3_gnn_sl2")):
            s_par.did(nc.sync.dma_start(dst[:, :], a[k]))
        s_par.did(nc.sync.dma_start(wrel[:, :, :], a["L3_gnn_w1"].rearrange("r d e -> d r e")))
        for n, k in (("L0_b_rel", "L0_gnn_b_rel"), ("L0_gamma", "L0_gnn_gamma"), ("L0_beta", "L0_gnn_beta")):
            s_par.did(nc.sync.dma_start(bcol[n][:, :], a[k].rearrange("(d a) -> d a", a=1)))
        s_par.did(nc.sync.dma_start(bcol["L2_att"][:, :], a["L2_gnn_att"].rearrange("h (c a) -> (h c) a", a=1)))
        for dst, k in ((bfull["L1_b0"], "L1_gnn_b0"), (bfull["L1_b1"], "L1_gnn_b1"),
                       (bfull["L3_b1"], "L3_gnn_b1"), (bfull["L3_b2"], "L3_gnn_b2"),
                       (b_sd[:, 0:P], "L2_gnn_b_src"), (b_sd[:, P:2 * P], "L2_gnn_b_dst"),
                       (bfull["L2_bias_out"], "L2_gnn_bias_out"), (bfull["L2_ln_gamma"], "L2_gnn_ln_gamma"),
                       (bfull["L2_ln_beta"], "L2_gnn_ln_beta")):
            s_par.did(nc.sync.dma_start(dst[:, :], a[k].rearrange("(a d) -> a d", a=1).to_broadcast([P, P])))

        G.did(G.after().memset(ident[:, :], 0.0))
        idn = G.did(G.after().affine_select(out=ident[:, :], in_=ident[:, :], compare_op=ALU.not_equal, fill=1.0,
                                            base=0, pattern=[[-1, P]], channel_multiplier=1))
        io = G.did(G.after().iota(iota_i[:, :], pattern=[[1, P]], base=0, channel_multiplier=0))
        G.did(G.after().memset(attm[:, :], 1.0))
        G.did(G.after().affine_select(out=attm[:, :], in_=attm[:, :], compare_op=ALU.is_ge, fill=0.0,
                                      base=0, pattern=[[-HD, HEADS]], channel_multiplier=1))
        am = G.did(G.after().affine_select(out=attm[:, :], in_=attm[:, :], compare_op=ALU.is_ge, fill=0.0,
                                           base=HD - 1, pattern=[[HD, HEADS]], channel_multiplier=-1))
        V.did(V.after(io).tensor_copy(iota[:, :], iota_i[:, :]))
        V.did(V.after(s_in.now()).scalar_tensor_tensor(out=relidx[:, 0:ET], in0=typ, scalar=float(NP),
                                                       in1=srcs[:, 0:ET], op0=ALU.mult, op1=ALU.add))
        tabled = V.did(V.after().tensor_tensor(rel[:, 0:ET], dcol, d0[:, 0:ET], ALU.subtract))
        V.did(V.after().scalar_tensor_tensor(out=d0two[:, :], in0=d0[0:1, 1:ET + U + 1], scalar=float(PAIR),
                                             in1=d0[0:1, 0:ET + U], op0=ALU.mult, op1=ALU.add))
        tabled = V.now()
        V.did(V.after(am, s_par.now()).tensor_scalar(attm[:, :], attm[:, :], bcol["L2_att"][:, 0:1], None, ALU.mult))
        V.did(V.after().tensor_tensor(fst[:, :], dstr["own"][:, :], dstr["prev"][:, :], ALU.not_equal))
        V.did(V.after().tensor_tensor(lst[:, :], dstr["own"][:, :], dstr["next"][:, :], ALU.not_equal))
        T.need(idn, s_par.now())
        for j, n in enumerate(raw):
            tw = T.did(nc.tensor.transpose(pb[4][:, j * P:(j + 1) * P], wraw[n], ident[:, :]))
        A.need(tw)
        for j, n in enumerate(raw):
            A.did(nc.scalar.activation(Wt[n][:, :], pb[4][:, j * P:(j + 1) * P], ACT.Copy))
        wt_ready = A.now()

        last_evac = {b: wt_ready for b in (4, 5, 6, 7)}
        rot = [0]

        def groups(per_bank=4):
            for g in range(0, NT, per_bank):
                b = 4 + rot[0] % 4
                rot[0] += 1
                yield b, list(range(g, min(g + per_bank, NT)))

        def turn(src_tiles, evac, *marks):
            T.need(*marks)
            for b, tiles in groups():
                T.need(last_evac[b])
                for j, t in enumerate(tiles):
                    m = T.did(nc.tensor.transpose(pb[b][:, j * P:(j + 1) * P], src_tiles(t), ident[:, :]))
                last_evac[b] = evac(pb[b][:, 0:len(tiles) * P], tiles, m)

        def product(terms, evac, *marks, per_bank=4):
            T.need(*marks)
            for b, tiles in groups(per_bank):
                T.need(last_evac[b])
                w = 512 // per_bank
                for j, t in enumerate(tiles):
                    for n, (lhs, rhs) in enumerate(terms):
                        m = nc.tensor.matmul(pb[b][:, j * w:(j + 1) * w], lhs[:, t * P:(t + 1) * P], rhs,
                                             start=(n == 0), stop=(n == len(terms) - 1))
                    m = T.did(m)
                last_evac[b] = evac(pb[b][:, 0:len(tiles) * w], tiles, m)

        def tiles_of(arr, tiles):
            return arr[:, tiles[0]:tiles[-1] + 1, :].rearrange("p t d -> p (t d)")

        def cols_of(arr, tiles):
            return arr[:, tiles[0] * P:(tiles[-1] + 1) * P]

        def to(dst, view, func=ACT.Copy):
            def evac(ps, tiles, m):
                A.need(m)
                return A.did(nc.scalar.activation(view(dst, tiles), ps, func))
            return evac

        def add_to_x(ps, tiles, m):
            V.after(m)
            xv = tiles_of(X, tiles)
            return V.did(nc.vector.tensor_tensor(xv, xv, ps, ALU.add))

        def plus_row(dst, row, then=None):
            def evac(ps, tiles, m):
                V.after(m)
                w = row.shape[1]
                rb = row[:, :].unsqueeze(1).to_broadcast([P, len(tiles), w])
                m = V.did(nc.vector.tensor_tensor(dst[:, tiles[0]:tiles[-1] + 1, :],
                                                  ps.rearrange("p (t d) -> p t d", d=w), rb, ALU.add))
                return then(tiles, m) if then else m
            return evac

        def plus_own(ps, tiles, m):
            V.after(m)
            m = V.did(nc.vector.tensor_tensor(tiles_of(H, tiles), ps, tiles_of(B1, tiles), ALU.add))
            A.did(A.after(m).activation(tiles_of(H, tiles), tiles_of(H, tiles), ACT.Relu))
            return m

        def bc(col):
            return col.unsqueeze(2).to_broadcast([P, NT, P])

        def normalise(src, dst):
            V.did(V.after().tensor_reduce(st["sum"][:, :], src[:, :, :], AX.X, ALU.add))
            V.did(V.after().tensor_scalar(st["mean"][:, :], st["sum"][:, :], 1.0 / P, None, ALU.mult))
            m = V.did(V.after().tensor_tensor(dst[:, :, :], src[:, :, :], bc(st["mean"][:, :]), ALU.subtract))
            m = A.did(A.after(m).activation(B1[:, :, :], dst[:, :, :], ACT.Square))
            V.did(V.after(m).tensor_reduce(st["var"][:, :], B1[:, :, :], AX.X, ALU.add))
            m = V.did(V.after().tensor_scalar(st["var"][:, :], st["var"][:, :], 1.0 / P, EPS, ALU.mult, ALU.add))
            m = A.did(A.after(m).activation(st["sd"][:, :], st["var"][:, :], ACT.Sqrt))
            return V.did(V.after(m).reciprocal(st["rstd"][:, :], st["sd"][:, :]))

        def pre_norm():
            normalise(X, H)
            return V.did(V.after().scalar_tensor_tensor(out=H[:, :, :], in0=H[:, :, :], scalar=0.0,
                                                        in1=bc(st["rstd"][:, :]), op0=ALU.max, op1=ALU.mult))

        s_tab = Dma(sem("s_tab"))

        def write_table(tab, src, mark):
            nc.sync.wait_ge(*mark)
            return s_tab.did(nc.sync.dma_start(tab.rearrange("(t p) d -> p t d", p=P), src[:, :, :]))

        def load_idx(table, g, col, eng=nc.sync):
            lo = 0 if g == 0 else GA
            return eng.dma_start(idx[g][:, :], table[:, bass.ds(col + lo, idx[g].shape[1])])

        def quiet(eng, s, n):
            eng.wait_ge(s, n)
            eng.sem_inc(s_tick, 1)

        def one_hot(k, col):
            return nc.vector.tensor_scalar(hot[:, k, :], iota[:, :], rel[:, bass.ds(col, 1)], None, ALU.is_equal)

        def first_hots():
            for k in range(LEAD):
                one_hot(k, k).then_inc(hot_n, 1)

        def clear_acc(n):
            ins = V.after().memset(acc[:, 0:n, 0:NP + P], 0.0)
            ins.then_inc(add_n, 1)
            cnt[add_n] += 1

        def first_nodes(eng, tile):
            pairs = d0two[0:1, bass.ds(tile, (U + 1) // 2, step=2)]
            _, two = nc.values_load_multi_w_load_instructions(pairs, engines=(eng,), min_val=0,
                                                              max_val=N * (PAIR + 1))
            return [v for w in two for v in (w % PAIR, w // PAIR)]

        def add_window(k, i, first, base, mmbase, n):
            nc.vector.wait_ge(mm_n, mmbase + i * U + (k + 1))
            nc.vector.wait_ge(add_n, base + i * U + k)
            av = acc[:, 0:n, bass.ds(first, P)]
            pv = pb[k % 4][:, 0:n * P].rearrange("p (a w) -> p a w", a=n)
            nc.vector.tensor_tensor(av, av, pv, ALU.add).then_inc(add_n, 1)

        def bank_free(k, i, base):
            nc.tensor.wait_ge(add_n, base + i * U + (k - 3 if k else 0))

        def first_idx(table, *marks):
            for m in marks:
                nc.sync.wait_ge(*m)
            nc.sync.wait_ge(mm_n, cnt[mm_n])
            for g in (0, 1):
                nc.sync.wait_ge(s_idx[g], cnt[s_idx[g]])
                load_idx(table, g, 0).then_inc(s_idx[g], 16)
                cnt[s_idx[g]] += 16

        def edge_sum(table, index, ready, with_degree=False, beside=None):
            n = 2 if with_degree else 1
            clear_acc(n)
            first_idx(index, tabled)
            nc.gpsimd.wait_ge(*ready)
            V.after()
            first_hots()
            if beside:
                beside()
            base = {s: cnt[s] for s in (hot_n, mm_n, add_n, *s_idx, *s_row)}
            with nc.Fori(0, IT, engines=(ENG.SP, ENG.Pool, ENG.PE, ENG.DVE)) as i:
                for g, last in ((0, GA), (1, U)):
                    quiet(nc.sync, mm_n, base[mm_n] + i * U + last)
                    load_idx(index, g, i * U + U).then_inc(s_idx[g], 16)
                for k in range(U):
                    g = int(k >= GA)
                    if k in (0, GA):
                        quiet(nc.gpsimd, s_idx[g], base[s_idx[g]] + i * 16)
                    c = k - GA * g
                    nc.gpsimd.indirect_dma_start(
                        rows[:, k, :], None, table[:, :],
                        bass.IndirectOffsetOnAxis(ap=idx[g][:, c:c + 1], axis=0)).then_inc(s_row[k], 16)
                first = first_nodes(ENG.DVE, i * U)
                for k in range(U):
                    nc.tensor.wait_ge(hot_n, base[hot_n] + i * U + (k + 1))
                    bank_free(k, i, base[add_n])
                    nc.tensor.wait_ge(s_row[k], base[s_row[k]] + i * 16 + 16)
                    m = nc.tensor.matmul(pb[k % 4][:, 0:P], rows[:, k, :], hot[:, k, :], start=True, stop=True)
                    if with_degree:
                        m = nc.tensor.matmul(pb[k % 4][:, P:2 * P], ones[:, :], hot[:, k, :], start=True, stop=True)
                    m.then_inc(mm_n, 1)
                    one_hot((k + LEAD) % U, i * U + (k + LEAD)).then_inc(hot_n, 1)
                    add_window(k, i, first[k], base[add_n], base[mm_n], n)
            cnt[hot_n] += ET + LEAD
            cnt[mm_n] += ET
            cnt[add_n] += ET
            for s in s_idx + s_row:
                cnt[s] += 16 * IT
            V.need((add_n, cnt[add_n]), (hot_n, cnt[hot_n]))
            return (add_n, cnt[add_n])

        AT = acc[:, 0, 0:NP]
        DG = acc[:, 1, 0:NP]

        V.need(s_x.now())
        h = pre_norm()
        tab = write_table(tabs[0], H, h)
        turn(lambda t: H[:, t, :], to(HT, cols_of), h)
        summed = edge_sum(tabs[0], srcs, tab, with_degree=True)
        for c in range(NCH):
            b = 4 + c % 4
            T.need(last_evac[b], A.now(), summed)
            s = slice(c * CH, (c + 1) * CH)
            nc.tensor.matmul(pb[b][:, 0:CH], Wt["L0_rel"][:, :], AT[:, s], start=True, stop=False)
            m = T.did(nc.tensor.matmul(pb[b][:, 0:CH], Wt["L0_root"][:, :], HT[:, s], start=False, stop=True))
            A.need(m)
            last_evac[b] = A.did(nc.scalar.activation(B1T[:, s], pb[b][:, 0:CH], ACT.Identity,
                                                      bias=bcol["L0_b_rel"][:, 0:1]))
        uT = B1T[:, 0:N]
        V.did(V.after(A.now()).tensor_reduce(bn["sum"][:, :], uT, AX.X, ALU.add))
        V.did(V.after().tensor_scalar(bn["mean"][:, :], bn["sum"][:, :], 1.0 / N, None, ALU.mult))
        m = V.did(V.after().tensor_scalar(B1T[:, :], B1T[:, :], bn["mean"][:, 0:1], None, ALU.subtract))
        m = A.did(A.after(m, T.now()).activation(HT[:, 0:N], uT, ACT.Square))
        V.did(V.after(m).tensor_reduce(bn["ss"][:, :], HT[:, 0:N], AX.X, ALU.add))
        m = V.did(V.after().tensor_scalar(bn["var"][:, :], bn["ss"][:, :], 1.0 / N, EPS, ALU.mult, ALU.add))
        m = A.did(A.after(m).activation(bn["sd"][:, :], bn["var"][:, :], ACT.Sqrt))
        V.did(V.after(m).reciprocal(bn["rstd"][:, :], bn["sd"][:, :]))
        m = V.did(V.after().tensor_tensor(bn["scale"][:, :], bn["rstd"][:, :], bcol["L0_gamma"][:, :], ALU.mult))
        m = A.did(A.after(m).activation(HT[:, :], B1T[:, :], ACT.Relu, bias=bcol["L0_beta"][:, 0:1],
                                        scale=bn["scale"][:, 0:1]))
        turn(lambda t: HT[:, t * P:(t + 1) * P], add_to_x, m)

        h = pre_norm()
        A.need(T.now())
        tab = write_table(tabs[1], H, h)
        turn(lambda t: H[:, t, :], to(HT, cols_of), h)
        def own1():
            product([(HT, Wt["L1_s0"][:, :])], plus_row(B1, bfull["L1_b0"]), A.now())
            V.did(V.after().tensor_scalar(invdeg[:, :], DG, 1.0, None, ALU.max))
            V.did(V.after().reciprocal(invdeg[:, :], invdeg[:, :]))

        edge_sum(tabs[1], srcs, tab, beside=own1)
        m = V.did(V.after().tensor_tensor(AT, AT, invdeg[:, :], ALU.mult))
        V.need(tab)
        product([(AT, Wt["L1_n0"][:, :])], plus_own, m)
        tab = write_table(tabs[2], H, A.now())
        A.need(T.now())
        turn(lambda t: H[:, t, :], to(HT, cols_of), A.now())
        V.need(T.now())

        def own2():
            product([(HT, Wt["L1_s1"][:, :])], add_to_x, A.now())
            V.did(V.after().tensor_tensor(X[:, :, :], X[:, :, :],
                                          bfull["L1_b1"][:, :].unsqueeze(1).to_broadcast([P, NT, P]), ALU.add))

        edge_sum(tabs[2], srcs, tab, beside=own2)
        m = V.did(V.after().tensor_tensor(AT, AT, invdeg[:, :], ALU.mult))
        product([(AT, Wt["L1_n1"][:, :])], add_to_x, m)

        V.need(tab)
        h = pre_norm()
        A.need(T.now())
        turn(lambda t: H[:, t, :], to(HT, cols_of), h)
        both = acc[:, :, :].rearrange("p a w -> p (a w)")[:, 0:NT * 2 * P].rearrange("p (t d) -> p t d", d=2 * P)
        V.need(T.now())
        product([(HT, w_sd[:, :])], plus_row(both, b_sd), A.now(), per_bank=2)
        nc.sync.wait_ge(*V.now())
        s_tab.did(nc.sync.dma_start(xs_t.rearrange("(t p) d -> p t d", p=P), both[:, :, 0:P]))
        t2 = s_tab.did(nc.sync.dma_start(xd_t[0:NP, :].rearrange("(t p) d -> p t d", p=P), both[:, :, P:2 * P]))
        for s, lo, hi in ((s_save[0], 0, 64), (s_save[1], 64, 96), (s_lgout, 96, P)):
            nc.sync.dma_start(xd_t[NP + lo:NP + hi, :], ones[lo:hi, :]).then_inc(s, 16)
            cnt[s] += 16
            nc.sync.wait_ge(s, cnt[s])
        tab = s_tab.now()

        TS = [k % 2 for k in range(U - 1)] + [2]
        TB = [(0, 1, 5)[s] for s in TS]
        EB = [(2, 3, 6)[s] for s in TS]
        def load_window(k, tile):
            first = nc.sync.value_load(d0[0:1, bass.ds(tile, 1)], min_val=0, max_val=N)
            return nc.sync.dma_start(win[:, k, :], xd_t[bass.ds(first, P), :])

        first_idx(srcs, tab)
        nc.gpsimd.wait_ge(*tab)
        nc.tensor.wait_ge(*A.now())
        with nc.allow_non_contiguous_dma(reason="window rows"):
            for k in range(U):
                load_window(k, k).then_inc(s_win[k], 16)
                cnt[s_win[k]] += 16
        V.after()
        first_hots()
        base = dict(cnt)
        A.after()

        def turn_hot(k):
            nc.tensor.transpose(pb[TB[k]][:, 0:P], hot[:, k, :], ident[:, :]).then_inc(tr_n, 1)

        def copy_hot(k):
            nc.scalar.activation(hotT[:, k, :], pb[TB[k]][:, 0:P], ACT.Copy).then_inc(trc_n, 1)

        for k in (0, 1):
            nc.tensor.wait_ge(hot_n, base[hot_n] + k + 1)
            turn_hot(k)
        nc.scalar.wait_ge(tr_n, base[tr_n] + 1)
        copy_hot(0)
        with nc.Fori(0, IT, engines=(ENG.SP, ENG.Pool, ENG.PE, ENG.DVE, ENG.Activation)) as i:
            n0 = i * U
            first = first_nodes(ENG.SP, n0 + U)
            for k in range(U):
                quiet(nc.sync, mm_n, base[mm_n] + n0 + (k + 1))
                nc.sync.dma_start(win[:, k, :], xd_t[bass.ds(first[k], P), :]).then_inc(s_win[k], 16)
            quiet(nc.sync, lgc_n, base[lgc_n] + i + 1)
            nc.sync.dma_start(lg_e.rearrange("(t p) h -> p t h", p=P)[:, bass.ds(n0, U), :],
                              lgs[:, :].rearrange("p (k h) -> p k h", k=U)).then_inc(s_lgout, 16)
            for k in range(U):
                g = int(k >= GA)
                if k in (0, GA):
                    quiet(nc.gpsimd, s_idx[g], base[s_idx[g]] + i * 16)
                    quiet(nc.gpsimd, s_save[g], base[s_save[g]] + i * 16)
                c = k - GA * g
                nc.gpsimd.indirect_dma_start(
                    rows[:, k, :], None, xs_t[:, :],
                    bass.IndirectOffsetOnAxis(ap=idx[g][:, c:c + 1], axis=0)).then_inc(s_row[k], 16)
            def logits(j):
                nc.tensor.wait_ge(lk_n, base[lk_n] + n0 + (j + 1))
                nc.tensor.matmul(pb[4][:, j * HEADS:(j + 1) * HEADS], lk[:, TS[j], :], attm[:, :],
                                 start=True, stop=True).then_inc(lg_n, 1)

            for k in range(U):
                nc.tensor.wait_ge(hot_n, base[hot_n] + n0 + (k + 3))
                nc.tensor.wait_ge(trc_n, base[trc_n] + n0 + (k + 1))
                turn_hot((k + 2) % U)
                nc.scalar.wait_ge(tr_n, base[tr_n] + n0 + (k + 2))
                copy_hot((k + 1) % U)
                nc.tensor.wait_ge(s_win[k], base[s_win[k]] + i * 16)
                nc.tensor.wait_ge(lk_n, base[lk_n] + n0 + (k - 1))
                nc.tensor.matmul(pb[EB[k]][:, 0:P], win[:, k, :], hotT[:, k, :], start=True, stop=False)
                nc.tensor.wait_ge(s_row[k], base[s_row[k]] + i * 16 + 16)
                nc.tensor.matmul(pb[EB[k]][:, 0:P], rows[:, k, :], ident[:, :], start=False,
                                 stop=True).then_inc(mm_n, 1)
                nc.scalar.wait_ge(mm_n, base[mm_n] + n0 + (k + 1))
                nc.scalar.wait_ge(lk_n, base[lk_n] + n0 + (k - 1))
                nc.scalar.activation(rl[:, TS[k], :], pb[EB[k]][:, 0:P], ACT.Relu, scale=0.8).then_inc(rl_n, 1)
                if k in (GA - 1, U - 1):
                    g = int(k >= GA)
                    lo, hi = (0, GA) if g == 0 else (GA, U)
                    load_idx(srcs, g, n0 + U, nc.scalar).then_inc(s_idx[g], 16)
                    nc.scalar.dma_start(xs_e[bass.ds(i, 1), :, lo:hi, :].rearrange("i p k d -> (i p) (k d)"),
                                        rows[:, lo:hi, :].rearrange("p k d -> p (k d)")).then_inc(s_save[g], 16)
                nc.vector.wait_ge(tr_n, base[tr_n] + n0 + (k + 1))
                one_hot((k + LEAD) % U, n0 + (k + LEAD)).then_inc(hot_n, 1)
                nc.vector.wait_ge(rl_n, base[rl_n] + n0 + (k + 1))
                nc.vector.wait_ge(lg_n, base[lg_n] + n0 + (k - 1 if k > 1 else 0))
                nc.vector.scalar_tensor_tensor(out=lk[:, TS[k], :], in0=pb[EB[k]][:, 0:P], scalar=0.2,
                                               in1=rl[:, TS[k], :], op0=ALU.mult, op1=ALU.add).then_inc(lk_n, 1)
                if k == 2:
                    nc.tensor.wait_ge(lgc_n, base[lgc_n] + i)
                if k > 1:
                    logits(k - 2)
            logits(U - 2)
            logits(U - 1)
            nc.scalar.wait_ge(lg_n, base[lg_n] + n0 + U)
            nc.scalar.wait_ge(s_lgout, base[s_lgout] + i * 16)
            nc.scalar.activation(lgs[:, :], pb[4][:, 0:U * HEADS], ACT.Copy).then_inc(lgc_n, 1)
        for s in (mm_n, trc_n, rl_n, lk_n, lg_n):
            cnt[s] += ET
        cnt[hot_n] += ET + LEAD
        cnt[tr_n] += ET + 2
        cnt[trc_n] += 1
        cnt[lgc_n] += IT
        for s in (*s_idx, *s_row, *s_win, *s_save, s_lgout):
            cnt[s] += 16 * IT

        s_b = Dma(sem("s_softmax"))
        nc.sync.wait_ge(s_lgout, cnt[s_lgout])
        lgin = s_b.did(nc.sync.dma_start(lg[:, :, :], lg_e.rearrange("(p t) h -> p t h", p=P)))
        sm = acc[:, :, :].rearrange("p a w -> p (a w)")[:, 0:ET * HEADS].rearrange("p (t h) -> p t h", h=HEADS)
        fl = [B1T[:, 0:ET], B1T[:, ET:2 * ET]]
        tmp = B1T[:, 2 * ET:2 * ET + 1]

        def scan(v, f, n, heads, t, backward):
            def run(lo, step, num):
                if backward:
                    first = n - 1 - lo
                    return bass.ds(first - step * (num - 1), num, step=step) if step > 1 else slice(first - num + 1, first + 1)
                return bass.ds(lo, num, step=step) if step > 1 else slice(lo, lo + num)

            def combine(left, right, step, num):
                ls, rs = run(left, step, num), run(right, step, num)
                if heads:
                    fr = f[:, rs].unsqueeze(2).to_broadcast([v.shape[0], num, HEADS])
                    vl, vr, tt = v[:, ls, :], v[:, rs, :], t[:, 0:num, :]
                else:
                    fr, vl, vr, tt = f[:, rs], v[:, ls], v[:, rs], t[:, 0:num]
                V.did(V.after().scalar_tensor_tensor(out=tt, in0=fr, scalar=-BIG, in1=vl, op0=ALU.mult, op1=ALU.add))
                V.did(V.after().tensor_tensor(vr, vr, tt, ALU.max))
                V.did(V.after().tensor_tensor(f[:, rs], f[:, rs], f[:, ls], ALU.max))

            s = 1
            while 2 * s <= n:
                combine(s - 1, 2 * s - 1, 2 * s, n // (2 * s))
                s *= 2
            while s >= 1:
                num = (n - 3 * s) // (2 * s) + 1 if n >= 3 * s else 0
                if num > 0:
                    combine(2 * s - 1, 3 * s - 1, 2 * s, num)
                s //= 2

        def carry(v, f, backward):
            e = ET - 1 if not backward else 0
            V.did(V.after().tensor_copy(car[:, 0:HEADS], v[:, e, :]))
            m = V.did(V.after().tensor_copy(car[:, HEADS:2 * HEADS], f[:, e:e + 1].to_broadcast([P, HEADS])))
            T.need(m, idn)
            nc.tensor.transpose(pb[5][0:HEADS, 0:P], car[:, 0:HEADS], ident[:, :])
            m = T.did(nc.tensor.transpose(pb[5][0:HEADS, P:2 * P], car[:, HEADS:2 * HEADS], ident[:, :]))
            V.did(V.after(m).tensor_copy(cs[:, 0:2, :], pb[5][0:HEADS, 0:2 * P].rearrange("h (a p) -> h a p", a=2)))
            scan(cs[:, 0, :], cs[:, 1, :], P, False, cs[:, 2, :], backward)
            V.did(V.after().memset(cs[:, 3, :], -BIG))
            if backward:
                m = V.did(V.after().tensor_copy(cs[:, 3, 0:P - 1], cs[:, 0, 1:P]))
            else:
                m = V.did(V.after().tensor_copy(cs[:, 3, 1:P], cs[:, 0, 0:P - 1]))
            T.need(m)
            m = T.did(nc.tensor.transpose(pb[5][:, 0:HEADS], cs[:, 3, :], ident[0:HEADS, 0:HEADS]))
            V.did(V.after(m).tensor_copy(car[:, 0:HEADS], pb[5][:, 0:HEADS]))
            cb = car[:, 0:HEADS].unsqueeze(1).to_broadcast([P, ET, HEADS])
            V.did(V.after().scalar_tensor_tensor(out=sm, in0=f[:, 0:ET].unsqueeze(2).to_broadcast([P, ET, HEADS]),
                                                 scalar=-BIG, in1=cb, op0=ALU.mult, op1=ALU.add))
            V.did(V.after().tensor_tensor(v, v, sm, ALU.max))

        V.need(t2)
        V.did(V.after().tensor_copy(fl[0], fst[:, :]))
        V.did(V.after(lgin).tensor_copy(fl[1], lst[:, :]))
        lv = lg[:, :, :]
        scan(lv, fl[0], ET, True, sm, False)
        carry(lv, fl[0], False)
        scan(lv, fl[1], ET, True, sm, True)
        carry(lv, fl[1], True)
        nc.sync.wait_ge(*V.now())
        again = s_b.did(nc.sync.dma_start(sm, lg_e.rearrange("(p t) h -> p t h", p=P)))
        m = V.did(V.after(again).tensor_tensor(lv, sm, lv, ALU.subtract))
        m = A.did(A.after(m).activation(lv, lv, ACT.Exp))
        m = V.did(V.after(m).scalar_tensor_tensor(out=lv, in0=lst[:, :].unsqueeze(2).to_broadcast([P, ET, HEADS]),
                                                  scalar=1.0, in1=lv, op0=ALU.add, op1=ALU.mult))
        nc.sync.wait_ge(*m)
        s_b.did(nc.sync.dma_start(pr_e.rearrange("(p t) h -> p t h", p=P), lv))
        probs = s_b.now()

        clear_acc(2)
        nc.sync.wait_ge(*probs)
        for g in (0, 1):
            nc.sync.wait_ge(s_save[g], cnt[s_save[g]])
        nc.sync.wait_ge(lk_n, cnt[lk_n])
        nc.sync.wait_ge(mm_n, cnt[mm_n])
        for k in range(U):
            nc.gpsimd.wait_ge(s_win[k], cnt[s_win[k]])
        span = ((0, GA), (GA, U))

        def load_edges(g, it):
            lo, hi = span[g]
            nc.sync.dma_start(rows[:, lo:hi, :].rearrange("p k d -> p (k d)"),
                              xs_e[bass.ds(it, 1), :, lo:hi, :].rearrange("i p k d -> (i p) (k d)")
                              ).then_inc(s_xe[g], 16)
            nc.sync.dma_start(prob[:, lo:hi, :],
                              pr_e.rearrange("(t p) h -> p t h", p=P)[:, bass.ds(it * U + lo, hi - lo), :]
                              ).then_inc(s_lp[g], 16)

        for g in (0, 1):
            load_edges(g, 0)
            cnt[s_xe[g]] += 16
            cnt[s_lp[g]] += 16
        def square_hot(k, col):
            nc.scalar.activation(hot[:, k, :], iota[:, :], ACT.Square, bias=rel[:, bass.ds(col, 1)],
                                 scale=-1.0).then_inc(sq_n, 1)

        def relu_hot(k):
            nc.scalar.activation(hot[:, k, :], hot[:, k, :], ACT.Relu, bias=1.0, scale=-2.0).then_inc(hot_n, 1)

        A.need((tr_n, cnt[tr_n]))
        for k in range(LEAD):
            square_hot(k, k)
        nc.scalar.wait_ge(sq_n, cnt[sq_n] + LEAD)
        for k in range(LEAD):
            relu_hot(k)
        cnt[sq_n] += LEAD
        base = dict(cnt)

        def attend(i, load_next):
            for g in (0, 1):
                lo, hi = span[g]
                w = hi - lo
                quiet(nc.gpsimd, s_xe[g], base[s_xe[g]] + i * 16)
                quiet(nc.gpsimd, s_lp[g], base[s_lp[g]] + i * 16)
                quiet(nc.gpsimd, mm_n, base[mm_n] + i * U + (hi - U))
                pg = prob[:, lo:hi, :].rearrange("p k h -> p (k h)").unsqueeze(2).to_broadcast([P, w * HEADS, HD])
                nc.gpsimd.tensor_tensor(win[:, lo:hi, :].rearrange("p k (h c) -> p (k h) c", c=HD),
                                        rows[:, lo:hi, :].rearrange("p k (h c) -> p (k h) c", c=HD),
                                        pg, ALU.mult).then_inc(msg_n, 1)
                if load_next:
                    quiet(nc.sync, msg_n, base[msg_n] + i * 2 + (g + 1))
                    quiet(nc.sync, pb_n, base[pb_n] + i * 2 + (g + 1))
                    load_edges(g, i + 1)
            first = first_nodes(ENG.DVE, i * U)
            for k in range(U):
                g = int(k >= GA)
                if k in (0, 3):
                    ga = int(k > 0)
                    lo, hi = span[ga]
                    pg = prob[:, lo:hi, :].rearrange("p k h -> p (k h)").unsqueeze(2).to_broadcast(
                        [P, (hi - lo) * HEADS, HD])
                    nc.scalar.wait_ge(s_lp[ga], base[s_lp[ga]] + i * 16)
                    nc.scalar.wait_ge(mm_n, base[mm_n] + i * U + (hi - U))
                    nc.scalar.activation(pbc[:, lo:hi, :].rearrange("p k (h c) -> p (k h) c", c=HD), pg,
                                         ACT.Copy).then_inc(pb_n, 1)
                nc.scalar.wait_ge(mm_n, base[mm_n] + i * U + (k + LEAD - U + 1))
                square_hot((k + LEAD) % U, i * U + (k + LEAD))
                nc.scalar.wait_ge(sq_n, base[sq_n] + i * U + (k + 1))
                relu_hot((k + LEAD) % U)
                nc.tensor.wait_ge(hot_n, base[hot_n] + i * U + (k + 1))
                bank_free(k, i, base[add_n])
                if k in (0, GA):
                    nc.tensor.wait_ge(msg_n, base[msg_n] + i * 2 + (g + 1))
                    nc.tensor.wait_ge(pb_n, base[pb_n] + i * 2 + (g + 1))
                nc.tensor.matmul(pb[k % 4][:, 0:P], win[:, k, :], hot[:, k, :], start=True, stop=True)
                nc.tensor.matmul(pb[k % 4][:, P:2 * P], pbc[:, k, :], hot[:, k, :], start=True,
                                 stop=True).then_inc(mm_n, 1)
                add_window(k, i, first[k], base[add_n], base[mm_n], 2)

        with nc.Fori(0, IT - 1, engines=(ENG.SP, ENG.Pool, ENG.PE, ENG.DVE, ENG.Activation)) as i:
            attend(i, True)
        attend(IT - 1, False)
        cnt[hot_n] += ET + LEAD
        cnt[mm_n] += ET
        cnt[add_n] += ET
        cnt[sq_n] += ET
        cnt[msg_n] += 2 * IT
        cnt[pb_n] += 2 * IT
        for g in (0, 1):
            cnt[s_xe[g]] += 16 * (IT - 1)
            cnt[s_lp[g]] += 16 * (IT - 1)
        V.need((add_n, cnt[add_n]), (hot_n, cnt[hot_n]), (pb_n, cnt[pb_n]), (msg_n, cnt[msg_n]))
        rden = st["sd8"]
        done = (add_n, cnt[add_n])

        def to_rden(ps, tiles, m):
            V.after(m)
            d = ps.rearrange("p (t h c) -> p t h c", h=HEADS, c=HD)[:, :, :, 0]
            r8 = rden[:, tiles[0]:tiles[-1] + 1, :]
            V.did(nc.vector.tensor_scalar(r8, d, 1e-30, None, ALU.max))
            return V.did(V.after().reciprocal(r8, r8))

        def weigh(ps, tiles, m):
            V.after(m)
            k = len(tiles) * HEADS
            b1, hv = tiles_of(B1, tiles), tiles_of(H, tiles)
            rb = rden[:, tiles[0]:tiles[-1] + 1, :].rearrange("p t h -> p (t h)").unsqueeze(2).to_broadcast([P, k, HD])
            m = V.did(nc.vector.tensor_tensor(b1.rearrange("p (k c) -> p k c", c=HD),
                                              ps.rearrange("p (k c) -> p k c", c=HD), rb, ALU.mult))
            V.did(V.after().tensor_tensor(hv, hv, b1, ALU.add))
            return m

        turn(lambda t: DG[:, t * P:(t + 1) * P], to_rden, done)
        turn(lambda t: AT[:, t * P:(t + 1) * P], weigh, done)
        def bcr(n):
            return bfull[n][:, :].unsqueeze(1).to_broadcast([P, NT, P])

        V.did(V.after().tensor_tensor(H[:, :, :], H[:, :, :], bcr("L2_bias_out"), ALU.add))
        normalise(H, H)
        V.did(V.after().tensor_tensor(H[:, :, :], H[:, :, :], bc(st["rstd"][:, :]), ALU.mult))
        V.did(V.after().tensor_tensor(H[:, :, :], H[:, :, :], bcr("L2_ln_gamma"), ALU.mult))
        m = V.did(V.after().tensor_tensor(H[:, :, :], H[:, :, :], bcr("L2_ln_beta"), ALU.add))
        m = A.did(A.after(m).activation(H[:, :, :], H[:, :, :], ACT.Gelu))
        V.did(V.after(m).tensor_tensor(X[:, :, :], X[:, :, :], H[:, :, :], ALU.add))

        h = pre_norm()
        A.need(T.now())
        turn(lambda t: H[:, t, :], to(HT, cols_of), h)
        s_rt = [Dma(sem("s_rtabA")), Dma(sem("s_rtabB"))]
        wload = s_par.now()

        def relation_tables(*marks):
            T.need(*marks)
            for t in range(NT):
                sl = t % 2
                for half in (0, 1):
                    b = 4 + 2 * sl + half
                    T.need(last_evac[b])
                    m = T.did(nc.tensor.matmul(pb[b][:, :], HT[:, t * P:(t + 1) * P],
                                               wrel[:, 4 * half:4 * half + 4, :].rearrange("d r e -> d (r e)"),
                                               start=True, stop=True))
                    dst = stage[sl][:, 4 * half:4 * half + 4, :].rearrange("p r e -> p (r e)")
                    if half == 0:
                        A.need(m, s_rt[sl].now())
                        last_evac[b] = ma = A.did(nc.scalar.activation(dst, pb[b][:, :], ACT.Copy))
                    else:
                        V.need(m, s_rt[sl].now())
                        last_evac[b] = mv = V.did(nc.vector.tensor_copy(dst, pb[b][:, :]))
                nc.sync.wait_ge(*ma)
                nc.sync.wait_ge(*mv)
                s_rt[sl].did(nc.sync.dma_start(
                    rel_t.rearrange("(r t p) e -> t p r e", r=R, p=P)[t], stage[sl]))
            nc.gpsimd.wait_ge(*s_rt[0].now())
            V.need(s_rt[0].now(), s_rt[1].now())
            return s_rt[1].now()

        V.need((hot_n, cnt[hot_n]))
        ready = relation_tables(A.now(), s_par.now())
        wused = T.now()
        nc.sync.wait_ge(*wused)
        w2 = s_par.did(nc.sync.dma_start(wrel[:, :, :], a["L3_gnn_w2"].rearrange("r d e -> d r e")))
        V.need(s_rt[1].now())
        def own_into_b1(w, bias):
            return lambda: product([(HT, Wt[w][:, :])], plus_row(B1, bfull[bias]), A.now())

        m = edge_sum(rel_t, relidx, ready, beside=own_into_b1("L3_sl1", "L3_b1"))
        turn(lambda t: AT[:, t * P:(t + 1) * P], plus_own, m)
        A.need(T.now())
        turn(lambda t: H[:, t, :], to(HT, cols_of), A.now())
        A.need((mm_n, cnt[mm_n]))
        V.need((mm_n, cnt[mm_n]), T.now())
        ready = relation_tables(A.now(), w2)
        m = edge_sum(rel_t, relidx, ready, beside=own_into_b1("L3_sl2", "L3_b2"))

        def relu_to_x(ps, tiles, m):
            V.after(m)
            b1, xv = tiles_of(B1, tiles), tiles_of(X, tiles)
            m = V.did(nc.vector.tensor_tensor(b1, ps, b1, ALU.add))
            V.did(V.after().scalar_tensor_tensor(out=xv, in0=b1, scalar=0.0, in1=xv, op0=ALU.max, op1=ALU.add))
            return m

        turn(lambda t: AT[:, t * P:(t + 1) * P], relu_to_x, m)
        nc.sync.wait_ge(*V.now())
        s_out = Dma(sem("s_out"))
        s_out.did(nc.sync.dma_start(out[0:(NT - 1) * P, :].rearrange("(t p) d -> p t d", p=P), X[:, 0:NT - 1, :]))
        s_out.did(nc.sync.dma_start(out[(NT - 1) * P:N, :], X[0:LAST, NT - 1, :]))
        nc.sync.wait_ge(*s_out.now())
        for g in (0, 1):
            nc.sync.wait_ge(s_idx[g], cnt[s_idx[g]])


def kernel(**inputs):
    import numpy as np
    import concourse.bacc as bacc
    from concourse.bass_utils import run_bass_kernel_spmd

    pad = ET * P - E
    src, dst, typ = (np.ascontiguousarray(inputs[n]) for n in ("src", "dst", "edge_type_8"))
    src = np.concatenate([src, np.zeros(pad, src.dtype)])
    typ = np.concatenate([typ, np.zeros(pad, typ.dtype)])
    dst = np.concatenate([dst, np.full(pad, N, dst.dtype)])
    end = np.full(1, -1, dst.dtype)
    arrays = {
        "src_col": src.reshape(ET, P).T, "type_col": typ.reshape(ET, P).T, "dst_col": dst.reshape(ET, P).T,
        "dst_first": dst[::P][None, :], "dst_own": dst.reshape(P, ET),
        "dst_prev": np.concatenate([end, dst[:-1]]).reshape(P, ET),
        "dst_next": np.concatenate([dst[1:], end]).reshape(P, ET),
    }
    for n, v in inputs.items():
        if n not in ("src", "dst", "edge_type_8"):
            arrays[n] = v
    arrays = {n: np.ascontiguousarray(v) for n, v in arrays.items()}
    nc = bacc.Bacc("TRN2", target_bir_lowering=False, num_devices=1)
    aps = {n: nc.dram_tensor("in_" + n, v.shape, mybir.dt.from_np(v.dtype), kind="ExternalInput").ap()
           for n, v in arrays.items()}
    out = nc.dram_tensor("out", (N, P), F32, kind="ExternalOutput").ap()
    build(nc, aps, out)
    r = run_bass_kernel_spmd(nc, [{"in_" + n: v for n, v in arrays.items()}], core_ids=[0])
    return r.results[0]["out"]
```

```python
from contextlib import ExitStack

import concourse.bass as bass
from concourse import mybir

F32 = mybir.dt.float32
I32 = mybir.dt.int32
ALU = mybir.AluOpType
ACT = mybir.ActivationFunctionType
AX = mybir.AxisListType
ENG = mybir.EngineType

P = 128
N = 3125
E = 103125
NT = -(-N // P)
NP = NT * P
LAST = N - (NT - 1) * P
ET = -(-E // P)
U = 13
IT = ET // U
GROUPS = ((0, 7), (7, U))
BATCHES = ((0, 3), (3, 7), (7, 10), (10, U))
SPAN = ((0, 7), (7, U))
PAIR = 4096
W = PAIR + P
R = 8
HEADS = 8
HD = P // HEADS
NCH = 8
CH = NP // NCH
EPS = 1e-5
BIG = 1e30
LEAD = 4
assert N < PAIR and PAIR * (N + 1) < 1 << 24
assert ET % U == 0 and ET * P >= E and CH * 4 <= 2048


class Lane:

    def __init__(self, eng, sem):
        self.eng, self.sem, self.n = eng, sem, 0

    def after(self, *marks):
        if self.n:
            self.eng.wait_ge(self.sem, self.n)
        for sem, n in marks:
            self.eng.wait_ge(sem, n)
        return self.eng

    def need(self, *marks):
        for sem, n in marks:
            self.eng.wait_ge(sem, n)
        return self.eng

    def did(self, ins):
        ins.then_inc(self.sem, 1)
        self.n += 1
        return (self.sem, self.n)

    def now(self):
        return (self.sem, self.n)


class Dma:

    def __init__(self, sem):
        self.sem, self.n = sem, 0

    def did(self, ins):
        ins.then_inc(self.sem, 16)
        self.n += 16
        return (self.sem, self.n)

    def now(self):
        return (self.sem, self.n)


def build(nc, a, out):
    with ExitStack() as ctx:
        def sem(name):
            return ctx.enter_context(nc.semaphore(name))

        def sb(name, shape, dt=F32):
            return ctx.enter_context(nc.sbuf_tensor(name, shape, dt))

        V = Lane(nc.vector, sem("s_dve"))
        A = Lane(nc.scalar, sem("s_act"))
        T = Lane(nc.tensor, sem("s_pe"))
        G = Lane(nc.gpsimd, sem("s_pool"))

        s_tick = sem("s_tick")
        hot_n, mm_n, add_n = sem("s_onehot"), sem("s_product"), sem("s_added")
        tr_n, trc_n, rl_n, lk_n = sem("s_hotT"), sem("s_hotT_copied"), sem("s_relu"), sem("s_leaky")
        lg_n, lgc_n = sem("s_logits"), sem("s_logits_copied")
        s_idx = [sem(f"s_idx{g}") for g in range(len(GROUPS))]
        s_row = [sem(f"s_row{k}") for k in range(U)]
        s_win = [sem(f"s_win{k}") for k in range(U)]
        s_save = [sem(f"s_save{g}") for g in range(len(GROUPS))]
        s_lgout = sem("s_logits_out")
        s_lp = [sem("s_probA"), sem("s_probB")]
        s_xe = [sem("s_rowsA"), sem("s_rowsB")]
        msg_n, pb_n = sem("s_msg"), sem("s_pbc")
        cnt = {}
        START = 16
        for s in (s_lgout, *s_save, *s_idx, *s_row, *s_win, *s_lp, *s_xe):
            cnt[s] = 0
        for s in (hot_n, mm_n, add_n, tr_n, trc_n, rl_n, lk_n, lg_n, lgc_n, msg_n, pb_n):
            nc.vector.sem_inc(s, START)
            cnt[s] = START

        X = sb("X", [P, NT, P])
        H = sb("H", [P, NT, P])
        HT = sb("HT", [P, NP])
        B1 = sb("B1", [P, NT, P])
        B1T = B1[:, :, :].rearrange("p t d -> p (t d)")
        invdeg = sb("invdeg", [P, NP])
        acc = sb("acc", [P, 2, W])
        buffers = sb("edge_buffers", [P, 4, U, P])
        rows = buffers[:, 0]
        hot = buffers[:, 1]
        win = buffers[:, 2]
        pbc = buffers[:, 3]
        hotT = pbc
        srcs = sb("srcs", [P, ET + U], I32)
        relidx = sb("relidx", [P, ET + U], I32)
        rel = sb("rel", [P, ET + U])
        d0 = sb("d0", [P, ET + U + 1], I32)
        d0two = sb("d0two", [1, ET + U], I32)
        idx = [sb(f"idx{g}", [P, hi - lo], I32) for g, (lo, hi) in enumerate(GROUPS)]
        iota_i = sb("iota_i", [P, P], I32)
        iota = sb("iota", [P, P])
        ident = sb("ident", [P, P])
        ones = sb("ones", [P, P])
        Wt = {n: sb("w_" + n, [P, P]) for n in ("L0_rel", "L0_root", "L1_s0", "L1_n0", "L1_s1", "L1_n1",
                                                "L3_sl1", "L3_sl2")}
        wrel = sb("wrel", [P, R, P])
        bcol = {n: sb("c_" + n, [P, 1]) for n in ("L0_b_rel", "L0_gamma", "L0_beta", "L2_att")}
        bfull = {n: sb("f_" + n, [P, P]) for n in ("L1_b0", "L1_b1", "L3_b1", "L3_b2", "L2_bias_out",
                                                   "L2_ln_gamma", "L2_ln_beta")}
        w_sd = sb("w_sd", [P, 2 * P])
        b_sd = sb("b_sd", [P, 2 * P])
        attm = sb("attm", [P, HEADS])
        st = {n: sb("st_" + n, [P, NT]) for n in ("sum", "mean", "var", "sd", "rstd")}
        st["sd8"] = sb("st_rden", [P, NT, HEADS])
        bn = {n: sb("bn_" + n, [P, 1]) for n in ("sum", "mean", "ss", "var", "sd", "rstd", "scale")}
        rl = sb("rl", [P, 3, P])
        lk = sb("lk", [P, 3, P])
        lgs = sb("lgs", [P, U * HEADS])
        prob = sb("prob", [P, U, HEADS])
        lg = sb("lg", [P, ET, HEADS])
        fst = sb("fst", [P, ET])
        lst = sb("lst", [P, ET])
        dstr = {n: sb("dstr_" + n, [P, ET], I32) for n in ("own", "prev", "next")}
        car = sb("car", [P, 2 * HEADS])
        cs = sb("cs", [HEADS, 4, P])
        pb = [ctx.enter_context(nc.psum_tensor(f"bank{i}", [P, 512], F32)) for i in range(8)]
        stage = [b[:, 0:R, :] for b in (rows, hot, win, pbc)]

        def dram(name, shape):
            return nc.dram_tensor(name, shape, F32, kind="Internal").ap()

        tabs = [dram(f"tab{i}", [NP, P]) for i in range(3)]
        xs_t, xd_t = dram("xs_t", [NP, P]), dram("xd_t", [W, P])
        rel_t = dram("rel_t", [R * NP, P])
        xs_e = dram("xs_e", [IT, P, U, P])
        lg_e = dram("lg_e", [ET * P, HEADS])
        pr_e = dram("pr_e", [ET * P, HEADS])

        s_in = Dma(sem("s_in"))
        s_x = Dma(sem("s_x"))
        s_par = Dma(sem("s_par"))
        mz = V.did(V.after().memset(X[:, NT - 1, :], 0.0))
        mz2 = V.did(V.after().memset(srcs[:, ET:ET + U], 0))
        V.did(V.after().memset(rel[:, ET:ET + U], 0.0))
        V.did(V.after().memset(relidx[:, ET:ET + U], 0))
        d0z = V.did(V.after().memset(d0[:, ET:ET + U + 1], 0))
        onz = V.did(V.after().memset(ones[:, :], 1.0))
        nc.sync.wait_ge(*mz)
        s_x.did(nc.sync.dma_start(X[:, 0:NT - 1, :], a["x"][0:(NT - 1) * P, :].rearrange("(t p) d -> p t d", p=P)))
        s_x.did(nc.sync.dma_start(X[0:LAST, NT - 1, :], a["x"][(NT - 1) * P:N, :]))
        typ = B1T[:, 0:ET].bitcast(I32)
        dcol = B1T[:, ET:2 * ET].bitcast(I32)
        nc.sync.wait_ge(*d0z)
        s_in.did(nc.sync.dma_start(srcs[:, 0:ET], a["src_col"]))
        s_in.did(nc.sync.dma_start(typ, a["type_col"]))
        s_in.did(nc.sync.dma_start(dcol, a["dst_col"]))
        s_in.did(nc.sync.dma_start(d0[:, 0:ET], a["dst_first"].to_broadcast([P, ET])))
        for n in ("own", "prev", "next"):
            s_par.did(nc.sync.dma_start(dstr[n][:, :], a["dst_" + n]))
        raw = {"L1_s0": a["L1_gnn_W_self0"], "L1_n0": a["L1_gnn_W_neigh0"],
               "L1_s1": a["L1_gnn_W_self1"], "L1_n1": a["L1_gnn_W_neigh1"]}
        wraw = {n: win[:, j, :] for j, n in enumerate(raw)}
        for n, src in raw.items():
            s_par.did(nc.sync.dma_start(wraw[n], src))
        for dst, k in ((Wt["L0_rel"], "L0_gnn_W_rel"), (Wt["L0_root"], "L0_gnn_W_root"),
                       (w_sd[:, 0:P], "L2_gnn_W_src"), (w_sd[:, P:2 * P], "L2_gnn_W_dst"),
                       (Wt["L3_sl1"], "L3_gnn_sl1"), (Wt["L3_sl2"], "L3_gnn_sl2")):
            s_par.did(nc.sync.dma_start(dst[:, :], a[k]))
        s_par.did(nc.sync.dma_start(wrel[:, :, :], a["L3_gnn_w1"].rearrange("r d e -> d r e")))
        for n, k in (("L0_b_rel", "L0_gnn_b_rel"), ("L0_gamma", "L0_gnn_gamma"), ("L0_beta", "L0_gnn_beta")):
            s_par.did(nc.sync.dma_start(bcol[n][:, :], a[k].rearrange("(d a) -> d a", a=1)))
        s_par.did(nc.sync.dma_start(bcol["L2_att"][:, :], a["L2_gnn_att"].rearrange("h (c a) -> (h c) a", a=1)))
        for dst, k in ((bfull["L1_b0"], "L1_gnn_b0"), (bfull["L1_b1"], "L1_gnn_b1"),
                       (bfull["L3_b1"], "L3_gnn_b1"), (bfull["L3_b2"], "L3_gnn_b2"),
                       (b_sd[:, 0:P], "L2_gnn_b_src"), (b_sd[:, P:2 * P], "L2_gnn_b_dst"),
                       (bfull["L2_bias_out"], "L2_gnn_bias_out"), (bfull["L2_ln_gamma"], "L2_gnn_ln_gamma"),
                       (bfull["L2_ln_beta"], "L2_gnn_ln_beta")):
            s_par.did(nc.sync.dma_start(dst[:, :], a[k].rearrange("(a d) -> a d", a=1).to_broadcast([P, P])))

        G.did(G.after().memset(ident[:, :], 0.0))
        idn = G.did(G.after().affine_select(out=ident[:, :], in_=ident[:, :], compare_op=ALU.not_equal, fill=1.0,
                                            base=0, pattern=[[-1, P]], channel_multiplier=1))
        io = G.did(G.after().iota(iota_i[:, :], pattern=[[1, P]], base=0, channel_multiplier=0))
        G.did(G.after().memset(attm[:, :], 1.0))
        G.did(G.after().affine_select(out=attm[:, :], in_=attm[:, :], compare_op=ALU.is_ge, fill=0.0,
                                      base=0, pattern=[[-HD, HEADS]], channel_multiplier=1))
        am = G.did(G.after().affine_select(out=attm[:, :], in_=attm[:, :], compare_op=ALU.is_ge, fill=0.0,
                                           base=HD - 1, pattern=[[HD, HEADS]], channel_multiplier=-1))
        V.did(V.after(io).tensor_copy(iota[:, :], iota_i[:, :]))
        V.did(V.after(s_in.now()).scalar_tensor_tensor(out=relidx[:, 0:ET], in0=typ, scalar=float(NP),
                                                       in1=srcs[:, 0:ET], op0=ALU.mult, op1=ALU.add))
        tabled = V.did(V.after().tensor_tensor(rel[:, 0:ET], dcol, d0[:, 0:ET], ALU.subtract))
        V.did(V.after().scalar_tensor_tensor(out=d0two[:, :], in0=d0[0:1, 1:ET + U + 1], scalar=float(PAIR),
                                             in1=d0[0:1, 0:ET + U], op0=ALU.mult, op1=ALU.add))
        tabled = V.now()
        V.did(V.after(am, s_par.now()).tensor_scalar(attm[:, :], attm[:, :], bcol["L2_att"][:, 0:1], None, ALU.mult))
        V.did(V.after().tensor_tensor(fst[:, :], dstr["own"][:, :], dstr["prev"][:, :], ALU.not_equal))
        V.did(V.after().tensor_tensor(lst[:, :], dstr["own"][:, :], dstr["next"][:, :], ALU.not_equal))
        T.need(idn, s_par.now())
        for j, n in enumerate(raw):
            tw = T.did(nc.tensor.transpose(pb[4][:, j * P:(j + 1) * P], wraw[n], ident[:, :]))
        A.need(tw)
        for j, n in enumerate(raw):
            A.did(nc.scalar.activation(Wt[n][:, :], pb[4][:, j * P:(j + 1) * P], ACT.Copy))
        wt_ready = A.now()

        last_evac = {b: wt_ready for b in (4, 5, 6, 7)}
        rot = [0]

        def groups(per_bank=4):
            for g in range(0, NT, per_bank):
                b = 4 + rot[0] % 4
                rot[0] += 1
                yield b, list(range(g, min(g + per_bank, NT)))

        def turn(src_tiles, evac, *marks):
            T.need(*marks)
            for b, tiles in groups():
                T.need(last_evac[b])
                for j, t in enumerate(tiles):
                    m = T.did(nc.tensor.transpose(pb[b][:, j * P:(j + 1) * P], src_tiles(t), ident[:, :]))
                last_evac[b] = evac(pb[b][:, 0:len(tiles) * P], tiles, m)

        def product(terms, evac, *marks, per_bank=4):
            T.need(*marks)
            for b, tiles in groups(per_bank):
                T.need(last_evac[b])
                w = 512 // per_bank
                for j, t in enumerate(tiles):
                    for n, (lhs, rhs) in enumerate(terms):
                        m = nc.tensor.matmul(pb[b][:, j * w:(j + 1) * w], lhs[:, t * P:(t + 1) * P], rhs,
                                             start=(n == 0), stop=(n == len(terms) - 1))
                    m = T.did(m)
                last_evac[b] = evac(pb[b][:, 0:len(tiles) * w], tiles, m)

        def tiles_of(arr, tiles):
            return arr[:, tiles[0]:tiles[-1] + 1, :].rearrange("p t d -> p (t d)")

        def cols_of(arr, tiles):
            return arr[:, tiles[0] * P:(tiles[-1] + 1) * P]

        def to(dst, view, func=ACT.Copy):
            def evac(ps, tiles, m):
                A.need(m)
                return A.did(nc.scalar.activation(view(dst, tiles), ps, func))
            return evac

        def add_to_x(ps, tiles, m):
            V.after(m)
            xv = tiles_of(X, tiles)
            return V.did(nc.vector.tensor_tensor(xv, xv, ps, ALU.add))

        def plus_row(dst, row, then=None):
            def evac(ps, tiles, m):
                V.after(m)
                w = row.shape[1]
                rb = row[:, :].unsqueeze(1).to_broadcast([P, len(tiles), w])
                m = V.did(nc.vector.tensor_tensor(dst[:, tiles[0]:tiles[-1] + 1, :],
                                                  ps.rearrange("p (t d) -> p t d", d=w), rb, ALU.add))
                return then(tiles, m) if then else m
            return evac

        def plus_own(ps, tiles, m):
            V.after(m)
            m = V.did(nc.vector.tensor_tensor(tiles_of(H, tiles), ps, tiles_of(B1, tiles), ALU.add))
            A.did(A.after(m).activation(tiles_of(H, tiles), tiles_of(H, tiles), ACT.Relu))
            return m

        def bc(col):
            return col.unsqueeze(2).to_broadcast([P, NT, P])

        def normalise(src, dst):
            V.did(V.after().tensor_reduce(st["sum"][:, :], src[:, :, :], AX.X, ALU.add))
            V.did(V.after().tensor_scalar(st["mean"][:, :], st["sum"][:, :], 1.0 / P, None, ALU.mult))
            m = V.did(V.after().tensor_tensor(dst[:, :, :], src[:, :, :], bc(st["mean"][:, :]), ALU.subtract))
            m = A.did(A.after(m).activation(B1[:, :, :], dst[:, :, :], ACT.Square))
            V.did(V.after(m).tensor_reduce(st["var"][:, :], B1[:, :, :], AX.X, ALU.add))
            m = V.did(V.after().tensor_scalar(st["var"][:, :], st["var"][:, :], 1.0 / P, EPS, ALU.mult, ALU.add))
            m = A.did(A.after(m).activation(st["sd"][:, :], st["var"][:, :], ACT.Sqrt))
            return V.did(V.after(m).reciprocal(st["rstd"][:, :], st["sd"][:, :]))

        def pre_norm():
            normalise(X, H)
            return V.did(V.after().scalar_tensor_tensor(out=H[:, :, :], in0=H[:, :, :], scalar=0.0,
                                                        in1=bc(st["rstd"][:, :]), op0=ALU.max, op1=ALU.mult))

        s_tab = Dma(sem("s_tab"))

        def write_table(tab, src, mark):
            nc.sync.wait_ge(*mark)
            return s_tab.did(nc.sync.dma_start(tab.rearrange("(t p) d -> p t d", p=P), src[:, :, :]))

        def load_idx(table, g, col, eng=nc.sync):
            lo, hi = GROUPS[g]
            return eng.dma_start(idx[g][:, :], table[:, bass.ds(col + lo, hi - lo)])

        def group_of(k):
            return next(g for g, (lo, hi) in enumerate(GROUPS) if lo <= k < hi)

        def quiet(eng, s, n):
            eng.wait_ge(s, n)
            eng.sem_inc(s_tick, 1)

        def one_hot(k, col):
            return nc.vector.tensor_scalar(hot[:, k, :], iota[:, :], rel[:, bass.ds(col, 1)], None, ALU.is_equal)

        def first_hots():
            for k in range(LEAD):
                one_hot(k, k).then_inc(hot_n, 1)

        def clear_acc(n):
            ins = V.after().memset(acc[:, 0:n, 0:NP + P], 0.0)
            ins.then_inc(add_n, 1)
            cnt[add_n] += 1

        def first_nodes(eng, tile):
            pairs = d0two[0:1, bass.ds(tile, (U + 1) // 2, step=2)]
            _, two = nc.values_load_multi_w_load_instructions(pairs, engines=(eng,), min_val=0,
                                                              max_val=N * (PAIR + 1))
            return [v for w in two for v in (w % PAIR, w // PAIR)]

        def add_window(k, i, first, base, mmbase, n):
            nc.vector.wait_ge(mm_n, mmbase + i * U + (k + 1))
            nc.vector.wait_ge(add_n, base + i * U + k)
            av = acc[:, 0:n, bass.ds(first, P)]
            pv = pb[k % 4][:, 0:n * P].rearrange("p (a w) -> p a w", a=n)
            nc.vector.tensor_tensor(av, av, pv, ALU.add).then_inc(add_n, 1)

        def bank_free(k, i, base):
            nc.tensor.wait_ge(add_n, base + i * U + (k - 3 if k else 0))

        def first_idx(table, *marks):
            for m in marks:
                nc.sync.wait_ge(*m)
            nc.sync.wait_ge(mm_n, cnt[mm_n])
            for g in range(len(GROUPS)):
                nc.sync.wait_ge(s_idx[g], cnt[s_idx[g]])
                load_idx(table, g, 0).then_inc(s_idx[g], 16)
                cnt[s_idx[g]] += 16

        def edge_sum(table, index, ready, with_degree=False, beside=None):
            n = 2 if with_degree else 1
            clear_acc(n)
            first_idx(index, tabled)
            nc.gpsimd.wait_ge(*ready)
            V.after()
            first_hots()
            if beside:
                beside()
            base = {s: cnt[s] for s in (hot_n, mm_n, add_n, *s_idx, *s_row)}
            with nc.Fori(0, IT, engines=(ENG.SP, ENG.Pool, ENG.PE, ENG.DVE)) as i:
                for g, (lo, hi) in enumerate(GROUPS):
                    quiet(nc.sync, mm_n, base[mm_n] + i * U + hi)
                    load_idx(index, g, i * U + U).then_inc(s_idx[g], 16)
                for k in range(U):
                    g = group_of(k)
                    c = k - GROUPS[g][0]
                    if c == 0:
                        quiet(nc.gpsimd, s_idx[g], base[s_idx[g]] + i * 16)
                    nc.gpsimd.indirect_dma_start(
                        rows[:, k, :], None, table[:, :],
                        bass.IndirectOffsetOnAxis(ap=idx[g][:, c:c + 1], axis=0)).then_inc(s_row[k], 16)
                first = first_nodes(ENG.DVE, i * U)
                for k in range(U):
                    nc.tensor.wait_ge(hot_n, base[hot_n] + i * U + (k + 1))
                    bank_free(k, i, base[add_n])
                    nc.tensor.wait_ge(s_row[k], base[s_row[k]] + i * 16 + 16)
                    m = nc.tensor.matmul(pb[k % 4][:, 0:P], rows[:, k, :], hot[:, k, :], start=True, stop=True)
                    if with_degree:
                        m = nc.tensor.matmul(pb[k % 4][:, P:2 * P], ones[:, :], hot[:, k, :], start=True, stop=True)
                    m.then_inc(mm_n, 1)
                    one_hot((k + LEAD) % U, i * U + (k + LEAD)).then_inc(hot_n, 1)
                    add_window(k, i, first[k], base[add_n], base[mm_n], n)
            cnt[hot_n] += ET + LEAD
            cnt[mm_n] += ET
            cnt[add_n] += ET
            for s in s_idx + s_row:
                cnt[s] += 16 * IT
            V.need((add_n, cnt[add_n]), (hot_n, cnt[hot_n]))
            return (add_n, cnt[add_n])

        AT = acc[:, 0, 0:NP]
        DG = acc[:, 1, 0:NP]

        V.need(s_x.now())
        h = pre_norm()
        tab = write_table(tabs[0], H, h)
        turn(lambda t: H[:, t, :], to(HT, cols_of), h)
        summed = edge_sum(tabs[0], srcs, tab, with_degree=True)
        for c in range(NCH):
            b = 4 + c % 4
            T.need(last_evac[b], A.now(), summed)
            s = slice(c * CH, (c + 1) * CH)
            nc.tensor.matmul(pb[b][:, 0:CH], Wt["L0_rel"][:, :], AT[:, s], start=True, stop=False)
            m = T.did(nc.tensor.matmul(pb[b][:, 0:CH], Wt["L0_root"][:, :], HT[:, s], start=False, stop=True))
            A.need(m)
            last_evac[b] = A.did(nc.scalar.activation(B1T[:, s], pb[b][:, 0:CH], ACT.Identity,
                                                      bias=bcol["L0_b_rel"][:, 0:1]))
        uT = B1T[:, 0:N]
        V.did(V.after(A.now()).tensor_reduce(bn["sum"][:, :], uT, AX.X, ALU.add))
        V.did(V.after().tensor_scalar(bn["mean"][:, :], bn["sum"][:, :], 1.0 / N, None, ALU.mult))
        m = V.did(V.after().tensor_scalar(B1T[:, :], B1T[:, :], bn["mean"][:, 0:1], None, ALU.subtract))
        m = A.did(A.after(m, T.now()).activation(HT[:, 0:N], uT, ACT.Square))
        V.did(V.after(m).tensor_reduce(bn["ss"][:, :], HT[:, 0:N], AX.X, ALU.add))
        m = V.did(V.after().tensor_scalar(bn["var"][:, :], bn["ss"][:, :], 1.0 / N, EPS, ALU.mult, ALU.add))
        m = A.did(A.after(m).activation(bn["sd"][:, :], bn["var"][:, :], ACT.Sqrt))
        V.did(V.after(m).reciprocal(bn["rstd"][:, :], bn["sd"][:, :]))
        m = V.did(V.after().tensor_tensor(bn["scale"][:, :], bn["rstd"][:, :], bcol["L0_gamma"][:, :], ALU.mult))
        m = A.did(A.after(m).activation(HT[:, :], B1T[:, :], ACT.Relu, bias=bcol["L0_beta"][:, 0:1],
                                        scale=bn["scale"][:, 0:1]))
        turn(lambda t: HT[:, t * P:(t + 1) * P], add_to_x, m)

        h = pre_norm()
        A.need(T.now())
        tab = write_table(tabs[1], H, h)
        turn(lambda t: H[:, t, :], to(HT, cols_of), h)
        def own1():
            product([(HT, Wt["L1_s0"][:, :])], plus_row(B1, bfull["L1_b0"]), A.now())
            V.did(V.after().tensor_scalar(invdeg[:, :], DG, 1.0, None, ALU.max))
            V.did(V.after().reciprocal(invdeg[:, :], invdeg[:, :]))

        edge_sum(tabs[1], srcs, tab, beside=own1)
        m = V.did(V.after().tensor_tensor(AT, AT, invdeg[:, :], ALU.mult))
        V.need(tab)
        product([(AT, Wt["L1_n0"][:, :])], plus_own, m)
        tab = write_table(tabs[2], H, A.now())
        A.need(T.now())
        turn(lambda t: H[:, t, :], to(HT, cols_of), A.now())
        V.need(T.now())

        def own2():
            product([(HT, Wt["L1_s1"][:, :])], add_to_x, A.now())
            V.did(V.after().tensor_tensor(X[:, :, :], X[:, :, :],
                                          bfull["L1_b1"][:, :].unsqueeze(1).to_broadcast([P, NT, P]), ALU.add))

        edge_sum(tabs[2], srcs, tab, beside=own2)
        m = V.did(V.after().tensor_tensor(AT, AT, invdeg[:, :], ALU.mult))
        product([(AT, Wt["L1_n1"][:, :])], add_to_x, m)

        V.need(tab)
        h = pre_norm()
        A.need(T.now())
        turn(lambda t: H[:, t, :], to(HT, cols_of), h)
        both = acc[:, :, :].rearrange("p a w -> p (a w)")[:, 0:NT * 2 * P].rearrange("p (t d) -> p t d", d=2 * P)
        V.need(T.now())
        product([(HT, w_sd[:, :])], plus_row(both, b_sd), A.now(), per_bank=2)
        nc.sync.wait_ge(*V.now())
        s_tab.did(nc.sync.dma_start(xs_t.rearrange("(t p) d -> p t d", p=P), both[:, :, 0:P]))
        t2 = s_tab.did(nc.sync.dma_start(xd_t[0:NP, :].rearrange("(t p) d -> p t d", p=P), both[:, :, P:2 * P]))
        for q, s in enumerate((*s_save, s_lgout)):
            lo, hi = q * P // (len(s_save) + 1), (q + 1) * P // (len(s_save) + 1)
            nc.sync.dma_start(xd_t[NP + lo:NP + hi, :], ones[lo:hi, :]).then_inc(s, 16)
            cnt[s] += 16
            nc.sync.wait_ge(s, cnt[s])
        tab = s_tab.now()

        TS = [k % 2 for k in range(U - 1)] + [2]
        TB = [(0, 1, 5)[s] for s in TS]
        EB = [(2, 3, 6)[s] for s in TS]
        def load_window(k, tile):
            first = nc.sync.value_load(d0[0:1, bass.ds(tile, 1)], min_val=0, max_val=N)
            return nc.sync.dma_start(win[:, k, :], xd_t[bass.ds(first, P), :])

        first_idx(srcs, tab)
        nc.gpsimd.wait_ge(*tab)
        nc.tensor.wait_ge(*A.now())
        with nc.allow_non_contiguous_dma(reason="window rows"):
            for k in range(U):
                load_window(k, k).then_inc(s_win[k], 16)
                cnt[s_win[k]] += 16
        V.after()
        first_hots()
        V.did(V.after(T.now()).tensor_tensor(H[:, :, :], H[:, :, :],
                                             bfull["L2_bias_out"][:, :].unsqueeze(1).to_broadcast([P, NT, P]), ALU.add))
        base = dict(cnt)
        A.after()

        def turn_hot(k):
            nc.tensor.transpose(pb[TB[k]][:, 0:P], hot[:, k, :], ident[:, :]).then_inc(tr_n, 1)

        def copy_hot(k):
            nc.scalar.activation(hotT[:, k, :], pb[TB[k]][:, 0:P], ACT.Copy).then_inc(trc_n, 1)

        for k in (0, 1):
            nc.tensor.wait_ge(hot_n, base[hot_n] + k + 1)
            turn_hot(k)
        nc.scalar.wait_ge(tr_n, base[tr_n] + 1)
        copy_hot(0)
        with nc.Fori(0, IT, engines=(ENG.SP, ENG.Pool, ENG.PE, ENG.DVE, ENG.Activation)) as i:
            n0 = i * U
            first = first_nodes(ENG.SP, n0 + U)
            for lo, hi in BATCHES:
                quiet(nc.sync, mm_n, base[mm_n] + n0 + hi)
                for g in range(len(GROUPS)):
                    if hi == GROUPS[g][1]:
                        load_idx(srcs, g, n0 + U).then_inc(s_idx[g], 16)
                for k in range(lo, hi):
                    nc.sync.dma_start(win[:, k, :], xd_t[bass.ds(first[k], P), :]).then_inc(s_win[k], 16)
            quiet(nc.sync, lgc_n, base[lgc_n] + i + 1)
            nc.sync.dma_start(lg_e.rearrange("(t p) h -> p t h", p=P)[:, bass.ds(n0, U), :],
                              lgs[:, :].rearrange("p (k h) -> p k h", k=U)).then_inc(s_lgout, 16)
            for k in range(U):
                g = group_of(k)
                c = k - GROUPS[g][0]
                if c == 0:
                    quiet(nc.gpsimd, s_idx[g], base[s_idx[g]] + i * 16)
                    quiet(nc.gpsimd, s_save[g], base[s_save[g]] + i * 16)
                nc.gpsimd.indirect_dma_start(
                    rows[:, k, :], None, xs_t[:, :],
                    bass.IndirectOffsetOnAxis(ap=idx[g][:, c:c + 1], axis=0)).then_inc(s_row[k], 16)
            def logits(j):
                nc.tensor.wait_ge(lk_n, base[lk_n] + n0 + (j + 1))
                nc.tensor.matmul(pb[4][:, j * HEADS:(j + 1) * HEADS], lk[:, TS[j], :], attm[:, :],
                                 start=True, stop=True).then_inc(lg_n, 1)

            for k in range(U):
                nc.tensor.wait_ge(hot_n, base[hot_n] + n0 + (k + 3))
                nc.tensor.wait_ge(trc_n, base[trc_n] + n0 + (k + 1))
                turn_hot((k + 2) % U)
                nc.scalar.wait_ge(tr_n, base[tr_n] + n0 + (k + 2))
                copy_hot((k + 1) % U)
                nc.tensor.wait_ge(s_win[k], base[s_win[k]] + i * 16)
                nc.tensor.wait_ge(lk_n, base[lk_n] + n0 + (k - 1))
                nc.tensor.matmul(pb[EB[k]][:, 0:P], win[:, k, :], hotT[:, k, :], start=True, stop=False)
                nc.tensor.wait_ge(s_row[k], base[s_row[k]] + i * 16 + 16)
                nc.tensor.matmul(pb[EB[k]][:, 0:P], rows[:, k, :], ident[:, :], start=False,
                                 stop=True).then_inc(mm_n, 1)
                nc.scalar.wait_ge(mm_n, base[mm_n] + n0 + (k + 1))
                nc.scalar.wait_ge(lk_n, base[lk_n] + n0 + (k - 1))
                nc.scalar.activation(rl[:, TS[k], :], pb[EB[k]][:, 0:P], ACT.Relu, scale=0.8).then_inc(rl_n, 1)
                g = group_of(k)
                lo, hi = GROUPS[g]
                if k == hi - 1:
                    nc.scalar.dma_start(xs_e[bass.ds(i, 1), :, lo:hi, :].rearrange("i p k d -> (i p) (k d)"),
                                        rows[:, lo:hi, :].rearrange("p k d -> p (k d)")).then_inc(s_save[g], 16)
                nc.vector.wait_ge(tr_n, base[tr_n] + n0 + (k + 1))
                one_hot((k + LEAD) % U, n0 + (k + LEAD)).then_inc(hot_n, 1)
                nc.vector.wait_ge(rl_n, base[rl_n] + n0 + (k + 1))
                nc.vector.wait_ge(lg_n, base[lg_n] + n0 + (k - 1 if k > 1 else 0))
                nc.vector.scalar_tensor_tensor(out=lk[:, TS[k], :], in0=pb[EB[k]][:, 0:P], scalar=0.2,
                                               in1=rl[:, TS[k], :], op0=ALU.mult, op1=ALU.add).then_inc(lk_n, 1)
                if k == 2:
                    nc.tensor.wait_ge(lgc_n, base[lgc_n] + i)
                if k > 1:
                    logits(k - 2)
            logits(U - 2)
            logits(U - 1)
            nc.scalar.wait_ge(lg_n, base[lg_n] + n0 + U)
            nc.scalar.wait_ge(s_lgout, base[s_lgout] + i * 16)
            nc.scalar.activation(lgs[:, :], pb[4][:, 0:U * HEADS], ACT.Copy).then_inc(lgc_n, 1)
        for s in (mm_n, trc_n, rl_n, lk_n, lg_n):
            cnt[s] += ET
        cnt[hot_n] += ET + LEAD
        cnt[tr_n] += ET + 2
        cnt[trc_n] += 1
        cnt[lgc_n] += IT
        for s in (*s_idx, *s_row, *s_win, *s_save, s_lgout):
            cnt[s] += 16 * IT

        s_b = Dma(sem("s_softmax"))
        nc.sync.wait_ge(s_lgout, cnt[s_lgout])
        lgin = s_b.did(nc.sync.dma_start(lg[:, :, :], lg_e.rearrange("(p t) h -> p t h", p=P)))
        l2 = buffers[:, :, :, :].rearrange("p a k d -> p (a k d)")[:, 0:ET * HEADS].rearrange("p (t h) -> p t h", h=HEADS)
        nc.sync.wait_ge(lg_n, cnt[lg_n])
        for s in (*s_save, *s_win):
            nc.sync.wait_ge(s, cnt[s])
        nc.sync.wait_ge(hot_n, cnt[hot_n])
        s_again = Dma(sem("s_logits_again"))
        again = s_again.did(nc.sync.dma_start(l2, lg_e.rearrange("(p t) h -> p t h", p=P)))
        sm = acc[:, :, :].rearrange("p a w -> p (a w)")[:, 0:ET * HEADS].rearrange("p (t h) -> p t h", h=HEADS)
        fl = [B1T[:, 0:ET], B1T[:, ET:2 * ET]]

        def scan(v, f, heads, backward):
            turned = slice(None, None, -1) if backward else slice(None)
            fs = f[:, turned]
            for vs in [v[:, turned, h] for h in range(HEADS)] if heads else [v[:, turned]]:
                V.did(V.after().tensor_tensor_scan(vs, fs, vs, -BIG, ALU.add, ALU.max))
            V.did(V.after().tensor_tensor_scan(fs, fs, fs, 0.0, ALU.min, ALU.min))

        def carry(v, f, backward):
            e = ET - 1 if not backward else 0
            V.did(V.after().tensor_copy(car[:, 0:HEADS], v[:, e, :]))
            m = V.did(V.after().tensor_copy(car[:, HEADS:2 * HEADS], f[:, e:e + 1].to_broadcast([P, HEADS])))
            T.need(m, idn)
            nc.tensor.transpose(pb[5][0:HEADS, 0:P], car[:, 0:HEADS], ident[:, :])
            m = T.did(nc.tensor.transpose(pb[5][0:HEADS, P:2 * P], car[:, HEADS:2 * HEADS], ident[:, :]))
            V.did(V.after(m).tensor_copy(cs[:, 0:2, :], pb[5][0:HEADS, 0:2 * P].rearrange("h (a p) -> h a p", a=2)))
            scan(cs[:, 0, :], cs[:, 1, :], False, backward)
            V.did(V.after().memset(cs[:, 3, :], -BIG))
            if backward:
                m = V.did(V.after().tensor_copy(cs[:, 3, 0:P - 1], cs[:, 0, 1:P]))
            else:
                m = V.did(V.after().tensor_copy(cs[:, 3, 1:P], cs[:, 0, 0:P - 1]))
            T.need(m)
            m = T.did(nc.tensor.transpose(pb[5][:, 0:HEADS], cs[:, 3, :], ident[0:HEADS, 0:HEADS]))
            V.did(V.after(m).tensor_copy(car[:, 0:HEADS], pb[5][:, 0:HEADS]))
            cb = car[:, 0:HEADS].unsqueeze(1).to_broadcast([P, ET, HEADS])
            V.did(V.after().tensor_tensor(sm, cb, f.unsqueeze(2).to_broadcast([P, ET, HEADS]), ALU.add))
            V.did(V.after().tensor_tensor(v, v, sm, ALU.max))

        V.need(t2)
        V.did(V.after().tensor_scalar(fl[0], fst[:, :], -BIG, None, ALU.mult))
        V.did(V.after(lgin).tensor_scalar(fl[1], lst[:, :], -BIG, None, ALU.mult))
        lv = lg[:, :, :]
        scan(lv, fl[0], True, False)
        carry(lv, fl[0], False)
        scan(lv, fl[1], True, True)
        carry(lv, fl[1], True)
        scanned = V.now()
        m = V.did(V.after(again).tensor_tensor(lv, l2, lv, ALU.subtract))
        nc.gpsimd.wait_ge(*scanned)
        nc.gpsimd.memset(acc[:, :, 0:NP + P], 0.0).then_inc(add_n, 1)
        cnt[add_n] += 1
        m = A.did(A.after(m).activation(lv, lv, ACT.Exp))
        m = V.did(V.after(m).scalar_tensor_tensor(out=lv, in0=lst[:, :].unsqueeze(2).to_broadcast([P, ET, HEADS]),
                                                  scalar=1.0, in1=lv, op0=ALU.add, op1=ALU.mult))
        nc.sync.wait_ge(*m)
        s_b.did(nc.sync.dma_start(pr_e.rearrange("(p t) h -> p t h", p=P), lv))
        probs = s_b.now()

        nc.sync.wait_ge(*probs)
        for g in range(len(GROUPS)):
            nc.sync.wait_ge(s_save[g], cnt[s_save[g]])
        nc.sync.wait_ge(lk_n, cnt[lk_n])
        nc.sync.wait_ge(mm_n, cnt[mm_n])
        for k in range(U):
            nc.gpsimd.wait_ge(s_win[k], cnt[s_win[k]])
        def load_edges(g, it):
            lo, hi = SPAN[g]
            nc.sync.dma_start(rows[:, lo:hi, :].rearrange("p k d -> p (k d)"),
                              xs_e[bass.ds(it, 1), :, lo:hi, :].rearrange("i p k d -> (i p) (k d)")
                              ).then_inc(s_xe[g], 16)
            nc.sync.dma_start(prob[:, lo:hi, :],
                              pr_e.rearrange("(t p) h -> p t h", p=P)[:, bass.ds(it * U + lo, hi - lo), :]
                              ).then_inc(s_lp[g], 16)

        for g in (0, 1):
            load_edges(g, 0)
            cnt[s_xe[g]] += 16
            cnt[s_lp[g]] += 16
        V.after()
        first_hots()
        base = dict(cnt)

        def attend(i, load_next):
            for g in (0, 1):
                lo, hi = SPAN[g]
                w = hi - lo
                quiet(nc.gpsimd, s_xe[g], base[s_xe[g]] + i * 16)
                quiet(nc.gpsimd, s_lp[g], base[s_lp[g]] + i * 16)
                quiet(nc.gpsimd, mm_n, base[mm_n] + i * U + (hi - U))
                pg = prob[:, lo:hi, :].rearrange("p k h -> p (k h)").unsqueeze(2).to_broadcast([P, w * HEADS, HD])
                nc.gpsimd.tensor_tensor(win[:, lo:hi, :].rearrange("p k (h c) -> p (k h) c", c=HD),
                                        rows[:, lo:hi, :].rearrange("p k (h c) -> p (k h) c", c=HD),
                                        pg, ALU.mult).then_inc(msg_n, 1)
                if load_next:
                    quiet(nc.sync, msg_n, base[msg_n] + i * 2 + (g + 1))
                    quiet(nc.sync, pb_n, base[pb_n] + i * 2 + (g + 1))
                    load_edges(g, i + 1)
            first = first_nodes(ENG.DVE, i * U)
            for k in range(U):
                if k in (0, 3):
                    ga = int(k > 0)
                    lo, hi = SPAN[ga]
                    pg = prob[:, lo:hi, :].rearrange("p k h -> p (k h)").unsqueeze(2).to_broadcast(
                        [P, (hi - lo) * HEADS, HD])
                    nc.scalar.wait_ge(s_lp[ga], base[s_lp[ga]] + i * 16)
                    nc.scalar.wait_ge(mm_n, base[mm_n] + i * U + (hi - U))
                    nc.scalar.activation(pbc[:, lo:hi, :].rearrange("p k (h c) -> p (k h) c", c=HD), pg,
                                         ACT.Copy).then_inc(pb_n, 1)
                nc.tensor.wait_ge(hot_n, base[hot_n] + i * U + (k + 1))
                bank_free(k, i, base[add_n])
                if k in (0, SPAN[1][0]):
                    g = int(k > 0)
                    nc.tensor.wait_ge(msg_n, base[msg_n] + i * 2 + (g + 1))
                    nc.tensor.wait_ge(pb_n, base[pb_n] + i * 2 + (g + 1))
                nc.tensor.matmul(pb[k % 4][:, 0:P], win[:, k, :], hot[:, k, :], start=True, stop=True)
                nc.tensor.matmul(pb[k % 4][:, P:2 * P], pbc[:, k, :], hot[:, k, :], start=True,
                                 stop=True).then_inc(mm_n, 1)
                one_hot((k + LEAD) % U, i * U + (k + LEAD)).then_inc(hot_n, 1)
                add_window(k, i, first[k], base[add_n], base[mm_n], 2)

        with nc.Fori(0, IT - 1, engines=(ENG.SP, ENG.Pool, ENG.PE, ENG.DVE, ENG.Activation)) as i:
            attend(i, True)
        attend(IT - 1, False)
        cnt[hot_n] += ET + LEAD
        cnt[mm_n] += ET
        cnt[add_n] += ET
        cnt[msg_n] += 2 * IT
        cnt[pb_n] += 2 * IT
        for g in (0, 1):
            cnt[s_xe[g]] += 16 * (IT - 1)
            cnt[s_lp[g]] += 16 * (IT - 1)
        V.need((add_n, cnt[add_n]), (hot_n, cnt[hot_n]), (pb_n, cnt[pb_n]), (msg_n, cnt[msg_n]))
        rden = st["sd8"]
        done = (add_n, cnt[add_n])

        def to_rden(ps, tiles, m):
            V.after(m)
            d = ps.rearrange("p (t h c) -> p t h c", h=HEADS, c=HD)[:, :, :, 0]
            r8 = rden[:, tiles[0]:tiles[-1] + 1, :]
            V.did(nc.vector.tensor_scalar(r8, d, 1e-30, None, ALU.max))
            return V.did(V.after().reciprocal(r8, r8))

        def weigh(ps, tiles, m):
            V.after(m)
            k = len(tiles) * HEADS
            b1, hv = tiles_of(B1, tiles), tiles_of(H, tiles)
            rb = rden[:, tiles[0]:tiles[-1] + 1, :].rearrange("p t h -> p (t h)").unsqueeze(2).to_broadcast([P, k, HD])
            m = V.did(nc.vector.tensor_tensor(b1.rearrange("p (k c) -> p k c", c=HD),
                                              ps.rearrange("p (k c) -> p k c", c=HD), rb, ALU.mult))
            V.did(V.after().tensor_tensor(hv, hv, b1, ALU.add))
            return m

        turn(lambda t: DG[:, t * P:(t + 1) * P], to_rden, done)
        turn(lambda t: AT[:, t * P:(t + 1) * P], weigh, done)
        def bcr(n):
            return bfull[n][:, :].unsqueeze(1).to_broadcast([P, NT, P])

        normalise(H, H)
        V.did(V.after().tensor_tensor(H[:, :, :], H[:, :, :], bc(st["rstd"][:, :]), ALU.mult))
        V.did(V.after().tensor_tensor(H[:, :, :], H[:, :, :], bcr("L2_ln_gamma"), ALU.mult))
        m = V.did(V.after().tensor_tensor(H[:, :, :], H[:, :, :], bcr("L2_ln_beta"), ALU.add))
        m = A.did(A.after(m).activation(H[:, :, :], H[:, :, :], ACT.Gelu))
        V.did(V.after(m).tensor_tensor(X[:, :, :], X[:, :, :], H[:, :, :], ALU.add))

        h = pre_norm()
        A.need(T.now())
        turn(lambda t: H[:, t, :], to(HT, cols_of), h)
        s_rt = [Dma(sem(f"s_rtab{j}")) for j in range(len(stage))]
        wload = s_par.now()

        def relation_tables(*marks):
            T.need(*marks)
            for t in range(NT):
                sl = t % len(stage)
                for half in (0, 1):
                    b = 4 + 2 * (t % 2) + half
                    T.need(last_evac[b])
                    m = T.did(nc.tensor.matmul(pb[b][:, :], HT[:, t * P:(t + 1) * P],
                                               wrel[:, 4 * half:4 * half + 4, :].rearrange("d r e -> d (r e)"),
                                               start=True, stop=True))
                    dst = stage[sl][:, 4 * half:4 * half + 4, :].rearrange("p r e -> p (r e)")
                    if half == 0:
                        A.need(m, s_rt[sl].now())
                        last_evac[b] = ma = A.did(nc.scalar.activation(dst, pb[b][:, :], ACT.Copy))
                    else:
                        V.need(m, s_rt[sl].now())
                        last_evac[b] = mv = V.did(nc.vector.tensor_copy(dst, pb[b][:, :]))
                nc.sync.wait_ge(*ma)
                nc.sync.wait_ge(*mv)
                s_rt[sl].did(nc.sync.dma_start(
                    rel_t.rearrange("(r t p) e -> t p r e", r=R, p=P)[t], stage[sl]))
            for s in s_rt[1:]:
                nc.gpsimd.wait_ge(*s.now())
            V.need(s_rt[1].now())
            return s_rt[0].now()

        V.need((hot_n, cnt[hot_n]))
        ready = relation_tables(A.now(), s_par.now())
        wused = T.now()
        nc.sync.wait_ge(*wused)
        w2 = s_par.did(nc.sync.dma_start(wrel[:, :, :], a["L3_gnn_w2"].rearrange("r d e -> d r e")))
        def own_into_b1(w, bias):
            return lambda: product([(HT, Wt[w][:, :])], plus_row(B1, bfull[bias]), A.now())

        m = edge_sum(rel_t, relidx, ready, beside=own_into_b1("L3_sl1", "L3_b1"))
        turn(lambda t: AT[:, t * P:(t + 1) * P], plus_own, m)
        A.need(T.now())
        turn(lambda t: H[:, t, :], to(HT, cols_of), A.now())
        A.need((mm_n, cnt[mm_n]))
        V.need((mm_n, cnt[mm_n]), T.now())
        ready = relation_tables(A.now(), w2)
        m = edge_sum(rel_t, relidx, ready, beside=own_into_b1("L3_sl2", "L3_b2"))

        def relu_to_x(ps, tiles, m):
            V.after(m)
            b1, xv = tiles_of(B1, tiles), tiles_of(X, tiles)
            m = V.did(nc.vector.tensor_tensor(b1, ps, b1, ALU.add))
            V.did(V.after().scalar_tensor_tensor(out=xv, in0=b1, scalar=0.0, in1=xv, op0=ALU.max, op1=ALU.add))
            return m

        turn(lambda t: AT[:, t * P:(t + 1) * P], relu_to_x, m)
        nc.sync.wait_ge(*V.now())
        s_out = Dma(sem("s_out"))
        s_out.did(nc.sync.dma_start(out[0:(NT - 1) * P, :].rearrange("(t p) d -> p t d", p=P), X[:, 0:NT - 1, :]))
        s_out.did(nc.sync.dma_start(out[(NT - 1) * P:N, :], X[0:LAST, NT - 1, :]))
        nc.sync.wait_ge(*s_out.now())
        for g in range(len(GROUPS)):
            nc.sync.wait_ge(s_idx[g], cnt[s_idx[g]])


def kernel(**inputs):
    import numpy as np
    import concourse.bacc as bacc
    from concourse.bass_utils import run_bass_kernel_spmd

    pad = ET * P - E
    src, dst, typ = (np.ascontiguousarray(inputs[n]) for n in ("src", "dst", "edge_type_8"))
    src = np.concatenate([src, np.zeros(pad, src.dtype)])
    typ = np.concatenate([typ, np.zeros(pad, typ.dtype)])
    dst = np.concatenate([dst, np.full(pad, N, dst.dtype)])
    end = np.full(1, -1, dst.dtype)
    arrays = {
        "src_col": src.reshape(ET, P).T, "type_col": typ.reshape(ET, P).T, "dst_col": dst.reshape(ET, P).T,
        "dst_first": dst[::P][None, :], "dst_own": dst.reshape(P, ET),
        "dst_prev": np.concatenate([end, dst[:-1]]).reshape(P, ET),
        "dst_next": np.concatenate([dst[1:], end]).reshape(P, ET),
    }
    for n, v in inputs.items():
        if n not in ("src", "dst", "edge_type_8"):
            arrays[n] = v
    arrays = {n: np.ascontiguousarray(v) for n, v in arrays.items()}
    nc = bacc.Bacc("TRN2", target_bir_lowering=False, num_devices=1)
    aps = {n: nc.dram_tensor("in_" + n, v.shape, mybir.dt.from_np(v.dtype), kind="ExternalInput").ap()
           for n, v in arrays.items()}
    out = nc.dram_tensor("out", (N, P), F32, kind="ExternalOutput").ap()
    build(nc, aps, out)
    r = run_bass_kernel_spmd(nc, [{"in_" + n: v for n, v in arrays.items()}], core_ids=[0])
    return r.results[0]["out"]
```
